# Optimizing a Trainium2 kernel written in Bass

```python
import numpy as np
import jax
import jax.numpy as jnp

def _softmax(x, axis=-1):
    return jax.nn.softmax(x, axis=axis)

def _gelu(x):
    return jax.nn.gelu(x, approximate=True)

def _silu(x):
    return jax.nn.silu(x)

def _sigmoid(x):
    return jax.nn.sigmoid(x)

def _layernorm(x, axis=-1, eps=1e-05):
    m = jnp.mean(x, axis=axis, keepdims=True)
    v = jnp.var(x, axis=axis, keepdims=True)
    return (x - m) / jnp.sqrt(v + eps)

def _scatter_add(tgt, idx, src, axis=0):
    return tgt.at[idx].add(src)

def _segment_sum(src, seg, n):
    return jax.ops.segment_sum(src, seg, n)
kernel_name = 'mk_lm_tower_d1_tok_ids2048_r4_d24526'

def setup_inputs(seed: int=0):
    np.random.seed(seed)
    _w = jnp.asarray

    def _rec_inputs():
        import jax
        import jax.numpy as jnp
        _rk = jax.random.key(seed)
        x = jax.random.randint(jax.random.fold_in(_rk, 1), (16, 256), 0, 12500, jnp.int32)
        return x
    x = _rec_inputs()

    def _L0_tok_setup():
        import jax, jax.numpy as jnp
        import numpy as np
        import math
        VOCAB = 12500
        EMB_DIM = 75
        D_MODEL = 512
        BATCH = 4
        SEQ = 2048
        key = jax.random.key(seed)
        k1, k2, k3, k4 = jax.random.split(key, 4)
        x = jax.random.randint(k1, (BATCH, SEQ), 0, VOCAB, dtype=jnp.int64 if jax.config.jax_enable_x64 else jnp.int32)
        emb = jax.random.normal(k2, (VOCAB, EMB_DIM), dtype=jnp.float32)
        W = jax.random.normal(k3, (EMB_DIM, D_MODEL), dtype=jnp.float32) * (1.0 / math.sqrt(EMB_DIM))
        b = jax.random.normal(k4, (D_MODEL,), dtype=jnp.float32) * 0.01
        return {'x': x, 'emb': emb, 'W': W, 'b': b}
    _L0_tok_all = _L0_tok_setup()
    _L0_tok_in = {k: v for k, v in _L0_tok_all.items() if k in ('emb', 'W', 'b')}
    del _L0_tok_all

    def _L0_attn_setup():
        import jax, jax.numpy as jnp
        import numpy as np
        import math
        NUM_HEADS = 16
        KV_HEADS = 4
        WINDOW = 256

        def _alibi_slopes(n):
            start = 2.0 ** (-2.0 ** (-(math.log2(n) - 3)))
            return jnp.array([start * start ** i for i in range(n)], dtype=jnp.float32)
        key = jax.random.key(seed)
        k0, k1, k2, k3, k4 = jax.random.split(key, 5)
        B, S, H = (2, 512, 512)
        D = H // NUM_HEADS
        std = 0.02
        return {'hidden_states': jax.random.normal(k0, (B, S, H), dtype=jnp.float32), 'Wq': jax.random.normal(k1, (H, H), dtype=jnp.float32) * std, 'Wk': jax.random.normal(k2, (H, KV_HEADS * D), dtype=jnp.float32) * std, 'Wv': jax.random.normal(k3, (H, KV_HEADS * D), dtype=jnp.float32) * std, 'Wo': jax.random.normal(k4, (H, H), dtype=jnp.float32) * std}
    _L0_attn_all = _L0_attn_setup()
    _L0_attn_in = {k: v for k, v in _L0_attn_all.items() if k in ('Wq', 'Wk', 'Wv', 'Wo')}
    del _L0_attn_all

    def _L0_ffn_setup():
        import jax, jax.numpy as jnp
        import numpy as np
        TOPK = 4
        key = jax.random.key(seed)
        k_x, k_a, k_b, k_w, k_bias = jax.random.split(key, 5)
        b, s, h, j, a, r = (4, 512, 512, 512, 64, 16)
        x = jax.random.normal(k_x, (b, s, h), dtype=jnp.float32)
        A = jax.random.normal(k_a, (a, r, h), dtype=jnp.float32) * 0.02
        B = jax.random.normal(k_b, (a, j, r), dtype=jnp.float32) * 0.02
        W = jax.random.normal(k_w, (j, h), dtype=jnp.float32) * 0.02
        bias = jax.random.normal(k_bias, (j,), dtype=jnp.float32) * 0.02
        return {'x': x, 'A': A, 'B': B, 'W': W, 'bias': bias}
    _L0_ffn_all = _L0_ffn_setup()
    _L0_ffn_in = {k: v for k, v in _L0_ffn_all.items() if k in ('A', 'B', 'W', 'bias')}
    del _L0_ffn_all
    return {'x': x, 'L0_tok_emb': _L0_tok_in['emb'], 'L0_tok_W': _L0_tok_in['W'], 'L0_tok_b': _L0_tok_in['b'], 'L0_attn_Wq': _L0_attn_in['Wq'], 'L0_attn_Wk': _L0_attn_in['Wk'], 'L0_attn_Wv': _L0_attn_in['Wv'], 'L0_attn_Wo': _L0_attn_in['Wo'], 'L0_ffn_A': _L0_ffn_in['A'], 'L0_ffn_B': _L0_ffn_in['B'], 'L0_ffn_W': _L0_ffn_in['W'], 'L0_ffn_bias': _L0_ffn_in['bias']}

def reference(x, L0_tok_emb, L0_tok_W, L0_tok_b, L0_attn_Wq, L0_attn_Wk, L0_attn_Wv, L0_attn_Wo, L0_ffn_A, L0_ffn_B, L0_ffn_W, L0_ffn_bias):
    import jax
    import jax.numpy as jnp

    def _L0_tok_ref(x, emb, W, b):
        import jax, jax.numpy as jnp
        import numpy as np
        import math
        VOCAB = 12500
        EMB_DIM = 75
        D_MODEL = 512
        BATCH = 4
        SEQ = 2048
        vecs = emb[x]
        out = jnp.einsum('bse,ed->bsd', vecs, W) + b
        return out * jnp.sqrt(jnp.asarray(W.shape[1], dtype=out.dtype))

    def _L0_attn_ref(hidden_states, Wq, Wk, Wv, Wo):
        import jax, jax.numpy as jnp
        import numpy as np
        import math
        NUM_HEADS = 16
        KV_HEADS = 4
        WINDOW = 256

        def _alibi_slopes(n):
            start = 2.0 ** (-2.0 ** (-(math.log2(n) - 3)))
            return jnp.array([start * start ** i for i in range(n)], dtype=jnp.float32)
        B, S, H = hidden_states.shape
        D = H // NUM_HEADS
        g = NUM_HEADS // KV_HEADS
        q = (hidden_states @ Wq).reshape(B, S, NUM_HEADS, D).transpose(0, 2, 1, 3)
        k = (hidden_states @ Wk).reshape(B, S, KV_HEADS, D).transpose(0, 2, 1, 3)
        v = (hidden_states @ Wv).reshape(B, S, KV_HEADS, D).transpose(0, 2, 1, 3)
        k = jnp.repeat(k, g, axis=1)
        v = jnp.repeat(v, g, axis=1)
        i = jnp.arange(S)[:, None]
        j = jnp.arange(S)[None, :]
        dist = -jnp.clip(j - i, 0, None).astype(jnp.float32)
        alibi = dist[None, :, :] * _alibi_slopes(NUM_HEADS)[:, None, None]
        window = (j <= i) & (j >= i - WINDOW)
        sliding = jnp.where(window, 1.0, -1000000000.0).astype(jnp.float32)
        scores = jnp.einsum('bhqd,bhkd->bhqk', q, k) * (1.0 / math.sqrt(D))
        scores = scores + alibi[None] + sliding[None, None]
        scores = jnp.where((j > i)[None, None], -jnp.inf, scores)
        w = jax.nn.softmax(scores, axis=-1)
        out = jnp.einsum('bhqk,bhkd->bhqd', w, v)
        out = out.transpose(0, 2, 1, 3).reshape(B, S, H)
        return out @ Wo

    def _L0_ffn_ref(x, A, B, W, bias):
        import jax, jax.numpy as jnp
        import numpy as np
        TOPK = 4
        vecs = jnp.einsum('arh,bsh->bsar', A, x)
        arrows = jnp.linalg.norm(vecs, axis=-1)
        _, idx = jax.lax.top_k(arrows, TOPK)
        routes = jax.nn.one_hot(idx, arrows.shape[-1], dtype=x.dtype).sum(-2) / TOPK
        v = jnp.einsum('bsa,bsar->bsr', routes, vecs)
        delta = jnp.einsum('bsa,ajr,bsr->bsj', routes, B, v)
        base = jnp.einsum('bsh,jh->bsj', x, W) + bias
        return base + delta
    h = _L0_tok_ref(x, L0_tok_emb, L0_tok_W, L0_tok_b)
    h = h + _L0_attn_ref(_layernorm(h, axis=-1), L0_attn_Wq, L0_attn_Wk, L0_attn_Wv, L0_attn_Wo)
    h = h + _L0_ffn_ref(_layernorm(h, axis=-1), L0_ffn_A, L0_ffn_B, L0_ffn_W, L0_ffn_bias)
    return h

_drawn_inputs = setup_inputs


def setup_inputs(seed=0):
    import zlib

    import numpy as np

    out = dict(_drawn_inputs(seed))
    spreads = {}
    factors = {'L0_tok_b': 6.018,
     'L0_attn_Wq': 8.0,
     'L0_attn_Wk': 8.0,
     'L0_attn_Wv': 8.0,
     'L0_attn_Wo': 8.0,
     'L0_ffn_A': 8.0,
     'L0_ffn_B': 8.0,
     'L0_ffn_W': 2.835,
     'L0_ffn_bias': 64.0}
    for name, (base, spread) in spreads.items():
        noise = np.random.default_rng([zlib.crc32(name.encode()), seed]).standard_normal(out[name].shape)
        drawn = base * np.exp(spread * noise) if base else spread * noise
        out[name] = jnp.asarray(drawn.astype(out[name].dtype))
    for name, factor in factors.items():
        out[name] = (out[name] * factor).astype(out[name].dtype)
    return out
```

```python
from contextlib import ExitStack

import concourse.bass as bass
from concourse import mybir

F32 = mybir.dt.float32
F32R = mybir.dt.float32r
BF16 = mybir.dt.bfloat16
I32 = mybir.dt.int32
U32 = mybir.dt.uint32
ALU = mybir.AluOpType
ACT = mybir.ActivationFunctionType
AX = mybir.AxisListType

P = 128
HEADS = 16
KV = 4
GROUP = HEADS // KV
TOPK = 4
EPS = 1e-5
NEVER = -1e30
HUGE = 3e38


def tower_kernel(nc, ids, emb, w_tok, b_tok, w_q, w_k, w_v, w_o, a_t, b_t, w_t, bias, out):
    EMB = emb.shape[1]
    EA = EMB + 1
    D = w_tok.shape[1]
    DC = D // P
    NT = ids.shape[1]
    TT = 2
    S = TT * P
    NB = NT // TT
    HD = D // HEADS
    KD = KV * HD
    QKV = D + 2 * KD
    AR = a_t.shape[1]
    NA = AR // 16
    R = AR // NA
    RC = AR // P
    ROOT = float(D) ** 0.5
    QSCALE = float(HD) ** -0.5
    assert HD == 32 and KD == P and S == 256 and D == 512 and AR == 1024 and RC == 8
    QSTACK = 3 * HD
    STACK = QSTACK + 2

    with ExitStack() as ctx:
        def sb(name, shape, dt=F32):
            return ctx.enter_context(nc.sbuf_tensor(name, shape, dt))

        def psum(name, shape, dt=F32):
            return ctx.enter_context(nc.psum_tensor(name, shape, dt))

        def sem(name):
            return ctx.enter_context(nc.semaphore(name))

        ps_pair = psum("ps_pair", [P, 2, 512])
        ps_small = psum("ps_small", [P, 512])
        ps_od = psum("ps_od", [P, 512])
        ps_vec = psum("ps_vec", [P, 2, 512])
        ps_acc = psum("ps_acc", [P, 512])
        ps_turn = psum("ps_turn", [P, 512])

        ident = sb("ident", [P, P])
        mask = sb("mask", [P, S])
        ident_b = sb("ident_b", [P, P], BF16)
        mask_t = sb("mask_t", [P, P], BF16)
        ones = mask[:, 0:HD]
        minus_half = sb("minus_half", [P, TT])
        bias_rows = sb("bias_rows", [P, D])
        idx_all = sb("idx_all", [P, NT + TT], I32)
        idx_now = sb("idx_now", [P, TT], I32)

        shared_a = sb("shared_a", [P, 8 * D])
        stage = shared_a[:, :].rearrange("p (i n) -> p i n", i=2)
        squares = shared_a[:, 0:AR]
        routed = shared_a[:, AR:2 * AR]
        u = shared_a[:, 2 * AR:3 * AR]
        result = shared_a[:, 3 * AR:4 * AR].rearrange("p (t n) -> p t n", t=TT)
        shared_b = sb("shared_b", [P, 6 * D])
        w_qkv = shared_b[:, :].rearrange("p (c n) -> p c n", c=DC)
        h0 = shared_b[:, 0:TT * D].rearrange("p (t n) -> p t n", t=TT)
        h1 = shared_b[:, TT * D:2 * TT * D].rearrange("p (t n) -> p t n", t=TT)
        x = shared_b[:, 2 * TT * D:3 * TT * D].rearrange("p (t n) -> p t n", t=TT)
        prob0 = sb("prob0", [P, 2, GROUP, S])
        prob1 = sb("prob1", [P, 2, GROUP, P])
        w_emb = prob1[:, 0, :, :].rearrange("p g s -> p (g s)")
        wc = prob0[:, 0, :, :].rearrange("p g s -> p (g s)")[:, 0:D]
        wc_t = prob0[:, 1, :, :].rearrange("p g s -> p (g s)")[:, 0:D].rearrange("p (c n) -> p c n", c=DC)
        w_mean = sb("w_mean", [P, 2])
        we_h = sb("we_h", [P, D], F32R)
        we_l = sb("we_l", [P, D], F32R)
        m_h = sb("m_h", [P, QKV], F32R)
        m_l = sb("m_l", [P, QKV], F32R)
        wo_h = sb("wo_h", [P, DC * D], F32R)
        wo_l = sb("wo_l", [P, DC * D], F32R)
        at_h = sb("at_h", [P, DC * AR], F32R)
        at_l = sb("at_l", [P, DC * AR], F32R)
        wt_h = sb("wt_h", [P, DC * D], F32R)
        wt_l = sb("wt_l", [P, DC * D], F32R)
        bt_h = sb("bt_h", [P, RC * D], F32R)
        bt_l = sb("bt_l", [P, RC * D], F32R)

        e_tok = sb("e_tok", [P, TT, EA])
        e_scaled = sb("e_scaled", [P, TT, EA])
        et_h = sb("et_h", [P, S], F32R)
        et_l = sb("et_l", [P, S], F32R)
        e2_h = sb("e2_h", [P, S], F32R)
        e2_l = sb("e2_l", [P, S], F32R)
        stats = sb("stats", [P, TT, 6])
        mean_var = sb("mean_var", [P, TT, 2])
        var_eps = sb("var_eps", [P, TT])
        rstd = sb("rstd", [P, TT])
        q_h = sb("q_h", [P, KV, S], F32R)
        q_l = sb("q_l", [P, KV, S], F32R)
        k_h = sb("k_h", [P, S], F32R)
        k_l = sb("k_l", [P, S], F32R)
        q_stack = sb("q_stack", [P, GROUP, KV, S], F32R)
        k_stack = sb("k_stack", [P, KV, S], F32R)
        v_tok = sb("v_tok", [P, TT, KD])
        row_max = sb("row_max", [P, TT, HEADS])
        m_rows_h = sb("m_rows_h", [TT * HEADS, P], F32R)
        m_rows_l = sb("m_rows_l", [TT * HEADS, P], F32R)
        rden = sb("rden", [P, S])
        o_t = sb("o_t", [P, 2, S])
        ot_h, ot_l = q_h, q_l

        stats2 = sb("stats2", [P, TT, 6])
        mean_var2 = sb("mean_var2", [P, TT, 2])
        var_eps2 = sb("var_eps2", [P, TT])
        rstd2 = sb("rstd2", [P, TT])
        xt_h = sb("xt_h", [P, TT, DC, P], F32R)
        xt_l = sb("xt_l", [P, TT, DC, P], F32R)
        arrows = sb("arrows", [P, NA + TOPK])
        top8 = sb("top8", [P, 8])
        struck = sb("struck", [P, NA + TOPK])
        route = sb("route", [P, NA])
        v_sum = sb("v_sum", [P, R])
        ut_h = sb("ut_h", [P, RC, P], F32R)
        ut_l = sb("ut_l", [P, RC, P], F32R)

        passed = sem("passed")
        const_pool = sem("const_pool")
        const_dve = sem("const_dve")
        idx_in = sem("idx_in")
        small_in = sem("small_in")
        qkv_in = sem("qkv_in")
        bias_in = sem("bias_in")
        big_in = [sem("big_in0"), sem("big_in1")]
        set_dve = sem("set_dve")
        set_act = sem("set_act")
        set_pe = sem("set_pe")
        part_hi = sem("part_hi")
        part_lo = sem("part_lo")

        idx_ready = sem("idx_ready")
        gathered = sem("gathered")
        et_done = sem("et_done")
        eth_ready = sem("eth_ready")
        etl_ready = sem("etl_ready")
        h0_done = sem("h0_done")
        h0_ready = sem("h0_ready")
        dve_attn = sem("dve_attn")
        mv_ready = sem("mv_ready")
        eps_ready = sem("eps_ready")
        rstd_ready = sem("rstd_ready")
        e2_ready = sem("e2_ready")
        e2t_done = sem("e2t_done")
        e2h_ready = sem("e2h_ready")
        e2l_ready = sem("e2l_ready")
        k_done = sem("k_done")
        q_done = sem("q_done")
        v_done = sem("v_done")
        kh_ready = sem("kh_ready")
        kl_ready = sem("kl_ready")
        qh_ready = sem("qh_ready")
        ql_ready = sem("ql_ready")
        v_ready = sem("v_ready")
        stacked = sem("stacked")
        s_done = sem("s_done")
        max_ready = sem("max_ready")
        mt_done = sem("mt_done")
        mh_ready = sem("mh_ready")
        ml_ready = sem("ml_ready")
        m_stacked = sem("m_stacked")
        st_done = sem("st_done")
        exp_ready = sem("exp_ready")
        pv_done = sem("pv_done")
        rden_ready = sem("rden_ready")
        o_ready = sem("o_ready")
        oth_ready = sem("oth_ready")
        otl_ready = sem("otl_ready")
        wo_done = sem("wo_done")
        h1_ready = sem("h1_ready")
        stats2_ready = sem("stats2_ready")
        mv2_ready = sem("mv2_ready")
        eps2_ready = sem("eps2_ready")
        rstd2_ready = sem("rstd2_ready")
        x_ready = sem("x_ready")
        hb_ready = sem("hb_ready")

        xt_done = sem("xt_done")
        xh_ready = sem("xh_ready")
        xl_ready = sem("xl_ready")
        vec_done = sem("vec_done")
        sq_ready = sem("sq_ready")
        dve_route = sem("dve_route")
        route_ready = sem("route_ready")
        routed_ready = sem("routed_ready")
        vsum_ready = sem("vsum_ready")
        u_ready = sem("u_ready")
        ut_done = sem("ut_done")
        uth_ready = sem("uth_ready")
        utl_ready = sem("utl_ready")
        acc_done = sem("acc_done")
        result_ready = sem("result_ready")
        stored = [sem("stored0"), sem("stored1")]

        def after(eng, s, b, per, k):
            n = b * per + k
            if isinstance(n, int) and n <= 0:
                return
            eng.wait_ge(s, n)

        def after_apart(eng, s, b, per, k):
            after(eng, s, b, per, k)
            if not isinstance(b, int):
                eng.sem_inc(passed, 1)

        n_stack = 6 * GROUP * 16
        n_mrow = 2 * TT * 16

        pieces = []
        for weight, hi, lo, n in ((w_o, wo_h, wo_l, 1), (a_t, at_h, at_l, 2), (w_t, wt_h, wt_l, 1), (b_t, bt_h, bt_l, 2)):
            src = weight.rearrange("(c p) n -> p c n", p=P)
            c = src.shape[1] // n
            for i in range(n):
                w = 4 * D
                pieces.append((src[:, i * c:(i + 1) * c, :], hi[:, i * w:(i + 1) * w], lo[:, i * w:(i + 1) * w]))

        block = ctx.enter_context(nc.Block())

        @block.sync
        def _(sp):
            sp.dma_start(idx_all[:, 0:NT], ids).then_inc(idx_in, 16)
            sp.dma_start(w_emb[0:EMB, :], w_tok).then_inc(small_in, 16)
            sp.dma_start(w_emb[EMB:EA, :], b_tok.rearrange("(o n) -> o n", o=1)).then_inc(small_in, 16)
            sp.dma_start(w_qkv[:, :, 0:D], w_q.rearrange("(c p) n -> p c n", p=P)).then_inc(qkv_in, 16)
            sp.dma_start(w_qkv[:, :, D:D + KD], w_k.rearrange("(c p) n -> p c n", p=P)).then_inc(qkv_in, 16)
            sp.dma_start(w_qkv[:, :, D + KD:QKV], w_v.rearrange("(c p) n -> p c n", p=P)).then_inc(qkv_in, 16)
            sp.dma_start(bias_rows[:, :], bias.rearrange("(o n) -> o n", o=1).broadcast_to([P, D])).then_inc(bias_in, 16)

            def load_piece(i):
                if i >= 2:
                    sp.wait_ge(part_lo, i - 1)
                src = pieces[i][0]
                dst = stage[:, i % 2, :].rearrange("p (c n) -> p c n", n=src.shape[2])
                sp.dma_start(dst, src).then_inc(big_in[i % 2], 16)

            load_piece(0)
            load_piece(1)

            def stack_parts(b):
                after_apart(sp, st_done, b - 1, KV, KV)
                after(sp, kl_ready, b, 1, 1)
                for g in range(KV):
                    rows = slice(HD * g, HD * (g + 1))
                    for slot, part in ((0, k_h), (1, k_l), (2, k_h)):
                        sp.dma_start(k_stack[HD * slot:HD * (slot + 1), g, :].bitcast(F32),
                                     part[rows, :].bitcast(F32)).then_inc(stacked, 16)
                after(sp, ql_ready, b, 2, 2)
                for g in range(GROUP):
                    rows = slice(HD * g, HD * (g + 1))
                    for slot, part in ((0, q_h), (1, q_h), (2, q_l)):
                        sp.dma_start(q_stack[HD * slot:HD * (slot + 1), g, :, :].bitcast(F32),
                                     part[rows, :, :].bitcast(F32)).then_inc(stacked, 16)

            def stack_max(b):
                after(sp, ml_ready, b, 1, 1)
                for slot, part in enumerate((m_rows_h, m_rows_l)):
                    for t in range(TT):
                        row = q_stack[QSTACK + slot:QSTACK + slot + 1, :, :, t * P:(t + 1) * P]
                        sp.dma_start(row.rearrange("o g c q -> o (g c) q").bitcast(F32),
                                     part[HEADS * t:HEADS * (t + 1), :].bitcast(F32)).then_inc(m_stacked, 16)

            def store(f, t):
                after_apart(sp, result_ready, f, TT, t + 1)
                sp.dma_start(out[bass.ds(f * S + t * P, P), :], result[:, t, :]).then_inc(stored[t], 16)

            def iteration(b, f):
                if b is not None:
                    stack_parts(b)
                if f is not None:
                    store(f, 0)
                if b is not None:
                    stack_max(b)
                if f is not None:
                    store(f, 1)

            stack_parts(0)
            for i in range(2, len(pieces)):
                load_piece(i)
            stack_max(0)
            iteration(1, 0)
            with sp.Fori(2, NB) as b:
                iteration(b, b - 1)
            iteration(None, NB - 1)
            for t in range(TT):
                sp.wait_ge(stored[t], 16 * NB)

        @block.gpsimd
        def _(pool):
            nc.gpsimd.memset(ident[:, :], 0.0).then_inc(const_pool, 1)
            nc.gpsimd.memset(mask[:, :], 1.0).then_inc(const_pool, 1)
            nc.gpsimd.memset(minus_half[:, :], -0.5).then_inc(const_pool, 1)
            nc.gpsimd.memset(idx_all[:, NT:NT + TT], 0).then_inc(const_pool, 1)
            nc.gpsimd.memset(e_tok[:, :, EMB:EA], 1.0).then_inc(const_pool, 1)
            nc.gpsimd.memset(ident_b[:, :], 0.0).then_inc(const_pool, 1)
            nc.gpsimd.memset(mask_t[:, :], 0.0).then_inc(const_pool, 1)
            pool.wait_ge(const_pool, 7)
            nc.gpsimd.affine_select(out=ident_b[:, :], in_=ident_b[:, :], compare_op=ALU.not_equal, fill=1.0,
                                    base=0, pattern=[[-1, P]], channel_multiplier=1).then_inc(const_pool, 1)
            nc.gpsimd.affine_select(out=mask_t[:, :], in_=mask_t[:, :], compare_op=ALU.is_ge, fill=NEVER,
                                    base=0, pattern=[[1, P]], channel_multiplier=-1).then_inc(const_pool, 1)
            nc.gpsimd.affine_select(out=ident[:, :], in_=ident[:, :], compare_op=ALU.not_equal, fill=1.0,
                                    base=0, pattern=[[-1, P]], channel_multiplier=1).then_inc(const_pool, 1)
            nc.gpsimd.affine_select(out=mask[:, P:S], in_=mask[:, P:S], compare_op=ALU.is_ge, fill=NEVER,
                                    base=0, pattern=[[-1, P]], channel_multiplier=1).then_inc(const_pool, 1)

            def gather(b):
                after(pool, e2_ready, b - 1, TT, TT)
                after(pool, gathered, b - 1, 16 * TT, 16 * TT)
                nc.gpsimd.tensor_copy(idx_now[:, :], idx_all[:, bass.ds(b * TT, TT)]).then_inc(idx_ready, 1)
                after_apart(pool, idx_ready, b, 1, 1)
                for t in range(TT):
                    nc.gpsimd.indirect_dma_start(
                        out=e_tok[:, t, 0:EMB], out_offset=None, in_=emb,
                        in_offset=bass.IndirectOffsetOnAxis(ap=idx_now[:, t:t + 1].bitcast(U32), axis=0),
                    ).then_inc(gathered, 16)

            def rstd_attn(b):
                after_apart(pool, mv_ready, b, TT, TT)
                nc.gpsimd.tensor_scalar_add(var_eps[:, :], mean_var[:, :, 1], EPS).then_inc(eps_ready, 1)
                after(pool, eps_ready, b, 1, 1)
                nc.gpsimd.tensor_tensor(rstd[:, :], var_eps[:, :], minus_half[:, :], ALU.pow).then_inc(rstd_ready, 1)

            def o_lo(b, c):
                after(pool, oth_ready, b, KV, c + 1)
                nc.gpsimd.tensor_tensor(ot_l[:, c, :], o_t[:, c % 2, :], ot_h[:, c, :].bitcast(F32),
                                        ALU.subtract).then_inc(otl_ready, 1)

            def rstd_ffn(b, t):
                after_apart(pool, mv2_ready, b, TT, t + 1)
                nc.gpsimd.tensor_scalar_add(var_eps2[:, t:t + 1], mean_var2[:, t, 1:2], EPS).then_inc(eps2_ready, 1)
                after(pool, eps2_ready, b, TT, t + 1)
                nc.gpsimd.tensor_tensor(rstd2[:, t:t + 1], var_eps2[:, t:t + 1], minus_half[:, 0:1],
                                        ALU.pow).then_inc(rstd2_ready, 1)

            def add_bias(b, t):
                after(pool, stored[t], b, 16, 0)
                nc.gpsimd.tensor_tensor(result[:, t, :], h1[:, t, :], bias_rows[:, :], ALU.add).then_inc(hb_ready, 1)

            def spread(f, t):
                after(pool, vsum_ready, f, TT, t + 1)
                after(pool, ut_done, f, 2 * TT, 2 * t)
                nc.gpsimd.tensor_tensor(u[:, :].rearrange("p (a r) -> p a r", r=R),
                                        route[:, :].unsqueeze(2).broadcast_to([P, NA, R]),
                                        v_sum[:, :].unsqueeze(1).broadcast_to([P, NA, R]),
                                        ALU.mult).then_inc(u_ready, 1)

            def iteration(b, f):
                if b is not None:
                    rstd_attn(b)
                    gather(b + 1)
                if f is not None:
                    spread(f, 0)
                    spread(f, 1)
                if b is not None:
                    for c in range(KV):
                        o_lo(b, c)
                    for t in range(TT):
                        rstd_ffn(b, t)
                    for t in range(TT):
                        add_bias(b, t)

            pool.wait_ge(idx_in, 16)
            pool.wait_ge(bias_in, 16)
            gather(0)
            iteration(0, None)
            iteration(1, 0)
            with pool.Fori(2, NB) as b:
                iteration(b, b - 1)
            iteration(None, NB - 1)
            pool.wait_ge(gathered, (NB + 1) * 16 * TT)

        @block.scalar
        def _(act):
            def e_hi(b):
                after(act, et_done, b, 1, 1)
                nc.scalar.copy(et_h[0:EA, :], ps_small[0:EA, 0:S]).then_inc(eth_ready, 1)

            def h0_out(b):
                after(act, h1_ready, b - 1, TT, TT)
                for t in range(TT):
                    after(act, h0_done, b, TT, t + 1)
                    nc.scalar.mul(h0[:, t, :], ps_pair[:, t, :], ROOT).then_inc(h0_ready, 1)

            def e2_hi(b):
                after(act, e2t_done, b, 1, 1)
                nc.scalar.copy(e2_h[0:EA, :], ps_small[0:EA, 0:S]).then_inc(e2h_ready, 1)

            def qkv_hi(b):
                after(act, stacked, b - 1, n_stack, n_stack)
                after(act, k_done, b, 1, 1)
                nc.scalar.copy(k_h[:, :], ps_small[:, 0:S]).then_inc(kh_ready, 1)
                for i in range(2):
                    after(act, q_done, b, 2, i + 1)
                    nc.scalar.copy(q_h[:, 2 * i:2 * i + 2, :].rearrange("p c s -> p (c s)"),
                                   ps_pair[:, i, :]).then_inc(qh_ready, 1)
                after(act, pv_done, b - 1, KV, KV)
                after(act, v_done, b, 1, 1)
                nc.scalar.copy(v_tok[:, :, :], ps_od[:, :].rearrange("p (t n) -> p t n", t=TT)[:, :, KD:2 * KD]).then_inc(v_ready, 1)

            def m_hi(b):
                after(act, mt_done, b, 1, 1)
                nc.scalar.mul(m_rows_h[:, :], ps_small[0:TT * HEADS, 0:P], -1.0).then_inc(mh_ready, 1)

            def exps(b, c):
                after(act, pv_done, b, KV, c - 1)
                after(act, st_done, b, KV, c + 1)
                nc.scalar.activation(prob0[:, c % 2, :, :].rearrange("p g q -> p (g q)"),
                                     ps_pair[:, :, :].rearrange("p i q -> p (i q)"), ACT.Exp,
                                     bias=ones[:, 0:1]).then_inc(exp_ready, 1)
                nc.scalar.activation(prob1[:, c % 2, :, :].rearrange("p g q -> p (g q)"), ps_small[:, :], ACT.Exp,
                                     bias=ones[:, 0:1]).then_inc(exp_ready, 1)

            def o_hi(b, c):
                after(act, wo_done, b - 1, TT, TT)
                after(act, o_ready, b, KV, c + 1)
                nc.scalar.copy(ot_h[:, c, :], o_t[:, c % 2, :]).then_inc(oth_ready, 1)

            def x_hi(f, t):
                after(act, acc_done, f - 1, TT, t + 1)
                after(act, xt_done, f, TT, t + 1)
                nc.scalar.copy(xt_h[:, t, :, :].rearrange("p c s -> p (c s)"), ps_turn[:, :]).then_inc(xh_ready, 1)

            def square(f, t):
                after(act, routed_ready, f, TT, t)
                for n in range(2):
                    after(act, vec_done, f, 2 * TT, 2 * t + n + 1)
                    nc.scalar.activation(squares[:, n * 512:(n + 1) * 512], ps_vec[:, n, :], ACT.Square).then_inc(sq_ready, 1)

            def ut_hi(f, t, h):
                if h == 0:
                    after(act, acc_done, f, TT, t)
                after(act, ut_done, f, 2 * TT, 2 * t + h + 1)
                nc.scalar.copy(ut_h[:, 4 * h:4 * h + 4, :].rearrange("p c s -> p (c s)"), ps_turn[:, :]).then_inc(uth_ready, 1)

            def iteration(b, f):
                if b is not None:
                    e_hi(b)
                if f is not None:
                    x_hi(f, 0)
                if b is not None:
                    h0_out(b)
                if f is not None:
                    square(f, 0)
                    x_hi(f, 1)
                if b is not None:
                    e2_hi(b)
                    qkv_hi(b)
                if f is not None:
                    square(f, 1)
                    ut_hi(f, 0, 0)
                    ut_hi(f, 0, 1)
                if b is not None:
                    m_hi(b)
                    exps(b, 0)
                if f is not None:
                    ut_hi(f, 1, 0)
                if b is not None:
                    exps(b, 1)
                    o_hi(b, 0)
                if f is not None:
                    ut_hi(f, 1, 1)
                if b is not None:
                    exps(b, 2)
                    o_hi(b, 1)
                    exps(b, 3)
                    o_hi(b, 2)
                    o_hi(b, 3)

            act.wait_ge(small_in, 32)
            act.wait_ge(const_dve, 1)
            nc.scalar.copy(we_h[0:EA, :], w_emb[0:EA, :]).then_inc(set_act, 1)
            act.wait_ge(set_pe, 1)
            nc.scalar.copy(wc_t[:, :, 0:EA], ps_turn[:, :].rearrange("p (c n) -> p c n", c=DC)[:, :, 0:EA]).then_inc(set_act, 1)
            act.wait_ge(set_pe, 2)
            nc.scalar.mul(m_h[0:EA, 0:D], ps_vec[0:EA, 0, :], QSCALE).then_inc(set_act, 1)
            nc.scalar.copy(m_h[0:EA, D:QKV], ps_vec[0:EA, 1, 0:QKV - D]).then_inc(set_act, 1)

            e_hi(0)
            h0_out(0)
            e2_hi(0)
            qkv_hi(0)
            for i, (_, hi, _lo) in enumerate(pieces):
                act.wait_ge(big_in[i % 2], 16 * (i // 2 + 1))
                nc.scalar.copy(hi, stage[:, i % 2, :]).then_inc(part_hi, 1)
            m_hi(0)
            for c in range(KV):
                exps(0, c)
                if c:
                    o_hi(0, c - 1)
            o_hi(0, KV - 1)
            iteration(1, 0)
            with act.Fori(2, NB) as b:
                iteration(b, b - 1)
            iteration(None, NB - 1)

        @block.vector
        def _(dve):
            def e_lo(b):
                after(dve, eth_ready, b, 1, 1)
                nc.vector.tensor_tensor(et_l[0:EA, :], ps_small[0:EA, 0:S], et_h[0:EA, :].bitcast(F32),
                                        ALU.subtract).then_inc(etl_ready, 1)

            def norm_stats(b):
                for t in range(TT):
                    after(dve, h0_ready, b, TT, t + 1)
                    nc.vector.bn_stats(stats[:, t, :], h0[:, t, :]).then_inc(dve_attn, 1)
                for t in range(TT):
                    after_apart(dve, dve_attn, b, TT, t + 1)
                    nc.vector.bn_aggr(mean_var[:, t, :], stats[:, t, :]).then_inc(mv_ready, 1)

            def e_scale(b):
                after(dve, rstd_ready, b, 1, 1)
                for t in range(TT):
                    nc.vector.tensor_scalar(e_scaled[:, t, :], e_tok[:, t, :], rstd[:, t:t + 1], ROOT,
                                            ALU.mult, ALU.mult).then_inc(e2_ready, 1)

            def e2_lo(b):
                after(dve, e2h_ready, b, 1, 1)
                nc.vector.tensor_tensor(e2_l[0:EA, :], ps_small[0:EA, 0:S], e2_h[0:EA, :].bitcast(F32),
                                        ALU.subtract).then_inc(e2l_ready, 1)

            def qk_lo(b):
                after(dve, kh_ready, b, 1, 1)
                nc.vector.tensor_tensor(k_l[:, :], ps_small[:, 0:S], k_h[:, :].bitcast(F32),
                                        ALU.subtract).then_inc(kl_ready, 1)
                for i in range(2):
                    after(dve, qh_ready, b, 2, i + 1)
                    nc.vector.tensor_tensor(q_l[:, 2 * i:2 * i + 2, :].rearrange("p c s -> p (c s)"), ps_pair[:, i, :],
                                            q_h[:, 2 * i:2 * i + 2, :].rearrange("p c s -> p (c s)").bitcast(F32),
                                            ALU.subtract).then_inc(ql_ready, 1)

            def maxima(b, c):
                for g in range(GROUP):
                    n = GROUP * c + g
                    col = KV * g + c
                    after_apart(dve, s_done, b, HEADS, n + 1)
                    nc.vector.tensor_tensor_reduce(out=ps_pair[:, n % 2, 0:P], in0=ps_pair[:, n % 2, 0:P], in1=mask[:, P:S],
                                                   scale=1.0, scalar=-HUGE, op0=ALU.add, op1=ALU.max,
                                                   accum_out=row_max[:, 0, col:col + 1])
                    nc.vector.tensor_tensor_reduce(out=ps_pair[:, n % 2, S:2 * S], in0=ps_pair[:, n % 2, S:2 * S], in1=mask[:, :],
                                                   scale=1.0, scalar=-HUGE, op0=ALU.add, op1=ALU.max,
                                                   accum_out=row_max[:, 1, col:col + 1]).then_inc(max_ready, 1)

            def m_lo(b):
                after(dve, mh_ready, b, 1, 1)
                nc.vector.scalar_tensor_tensor(out=m_rows_l[:, :], in0=ps_small[0:TT * HEADS, 0:P], scalar=-1.0,
                                               in1=m_rows_h[:, :].bitcast(F32), op0=ALU.mult,
                                               op1=ALU.subtract).then_inc(ml_ready, 1)

            def normalise(b, c):
                after(dve, pv_done, b, KV, c + 1)
                nc.vector.reciprocal(rden[:, :], ps_od[:, S:2 * S]).then_inc(rden_ready, 1)
                after(dve, otl_ready, b, KV, c - 1)
                after(dve, rden_ready, b, KV, c + 1)
                nc.vector.tensor_tensor(o_t[:, c % 2, :], ps_od[:, 0:S], rden[:, :], ALU.mult).then_inc(o_ready, 1)

            def residual(b, t):
                after(dve, hb_ready, b - 1, TT, t + 1)
                after(dve, wo_done, b, TT, t + 1)
                nc.vector.tensor_tensor(h1[:, t, :], ps_acc[:, :], h0[:, t, :], ALU.add).then_inc(h1_ready, 1)
                after(dve, h1_ready, b, TT, t + 1)
                nc.vector.bn_stats(stats2[:, t, :], h1[:, t, :]).then_inc(stats2_ready, 1)
                after_apart(dve, stats2_ready, b, TT, t + 1)
                nc.vector.bn_aggr(mean_var2[:, t, :], stats2[:, t, :]).then_inc(mv2_ready, 1)

            def norm_x(b, t):
                after(dve, rstd2_ready, b, TT, t + 1)
                nc.vector.tensor_scalar(x[:, t, :], h1[:, t, :], mean_var2[:, t, 0:1], rstd2[:, t:t + 1],
                                        ALU.subtract, ALU.mult).then_inc(x_ready, 1)

            def x_lo(f, t):
                after(dve, xh_ready, f, TT, t + 1)
                nc.vector.tensor_tensor(xt_l[:, t, :, :].rearrange("p c s -> p (c s)"), ps_turn[:, :],
                                        xt_h[:, t, :, :].rearrange("p c s -> p (c s)").bitcast(F32),
                                        ALU.subtract).then_inc(xl_ready, 1)

            def routing(f, t):
                after(dve, sq_ready, f, 2 * TT, 2 * t + 2)
                nc.vector.tensor_reduce(out=arrows[:, 0:NA], in_=squares[:, :].rearrange("p (a r) -> p a r", r=R),
                                        axis=AX.X, op=ALU.add).then_inc(dve_route, 1)
                after_apart(dve, dve_route, f, 3 * TT, 3 * t + 1)
                nc.vector.max(out=top8[:, :], in_=arrows[:, :]).then_inc(dve_route, 1)
                after_apart(dve, dve_route, f, 3 * TT, 3 * t + 2)
                nc.vector.match_replace(out=struck[:, :], in_to_replace=top8[:, :], in_values=arrows[:, :],
                                        imm_value=-1.0).then_inc(dve_route, 1)
                after(dve, u_ready, f, TT, t)
                after(dve, dve_route, f, 3 * TT, 3 * t + 3)
                nc.vector.tensor_scalar(route[:, :], struck[:, 0:NA], -1.0, 1.0 / TOPK, ALU.is_equal,
                                        ALU.mult).then_inc(route_ready, 1)
                after(dve, route_ready, f, TT, t + 1)
                nc.vector.tensor_tensor(routed[:, :].rearrange("p (a r) -> p a r", r=R),
                                        ps_vec[:, :, :].rearrange("p i (a r) -> p (i a) r", r=R),
                                        route[:, :].unsqueeze(2).broadcast_to([P, NA, R]),
                                        ALU.mult).then_inc(routed_ready, 1)
                after(dve, routed_ready, f, TT, t + 1)
                nc.vector.tensor_reduce(out=v_sum[:, :], in_=routed[:, :].rearrange("p (a r) -> p r a", r=R),
                                        axis=AX.X, op=ALU.add).then_inc(vsum_ready, 1)

            def ut_lo(f, t, h):
                after(dve, uth_ready, f, 2 * TT, 2 * t + h + 1)
                nc.vector.tensor_tensor(ut_l[:, 4 * h:4 * h + 4, :].rearrange("p c s -> p (c s)"), ps_turn[:, :],
                                        ut_h[:, 4 * h:4 * h + 4, :].rearrange("p c s -> p (c s)").bitcast(F32),
                                        ALU.subtract).then_inc(utl_ready, 1)

            def finish(f, t):
                after(dve, hb_ready, f, TT, t + 1)
                after(dve, acc_done, f, TT, t + 1)
                nc.vector.tensor_tensor(result[:, t, :], ps_acc[:, :], result[:, t, :], ALU.add).then_inc(result_ready, 1)

            def iteration(b, f):
                if b is not None:
                    e_lo(b)
                if f is not None:
                    x_lo(f, 0)
                if b is not None:
                    norm_stats(b)
                if f is not None:
                    routing(f, 0)
                    x_lo(f, 1)
                if b is not None:
                    e_scale(b)
                    e2_lo(b)
                    qk_lo(b)
                if f is not None:
                    ut_lo(f, 0, 0)
                if b is not None:
                    maxima(b, 0)
                if f is not None:
                    ut_lo(f, 0, 1)
                if b is not None:
                    maxima(b, 1)
                if f is not None:
                    routing(f, 1)
                if b is not None:
                    maxima(b, 2)
                    maxima(b, 3)
                if f is not None:
                    finish(f, 0)
                if b is not None:
                    m_lo(b)
                if f is not None:
                    ut_lo(f, 1, 0)
                if b is not None:
                    normalise(b, 0)
                if f is not None:
                    ut_lo(f, 1, 1)
                if b is not None:
                    normalise(b, 1)
                    normalise(b, 2)
                if f is not None:
                    finish(f, 1)
                if b is not None:
                    normalise(b, 3)
                    for t in range(TT):
                        residual(b, t)
                    for t in range(TT):
                        norm_x(b, t)

            for m in (we_h, we_l, m_h, m_l, et_h, et_l, e2_h, e2_l):
                nc.vector.memset(m[64:P, :].bitcast(F32), 0.0)
            nc.vector.memset(arrows[:, NA:NA + TOPK], HUGE)
            nc.vector.memset(k_stack[QSTACK:P, :, :].bitcast(F32), 1.0).then_inc(const_dve, 1)
            dve.wait_ge(const_dve, 1)

            dve.wait_ge(set_act, 1)
            nc.vector.tensor_tensor(we_l[0:EA, :], w_emb[0:EA, :], we_h[0:EA, :].bitcast(F32), ALU.subtract).then_inc(set_dve, 1)
            nc.vector.tensor_reduce(out=w_mean[0:EA, 0:1], in_=w_emb[0:EA, :], axis=AX.X, op=ALU.add).then_inc(set_dve, 1)
            dve.wait_ge(set_dve, 2)
            nc.vector.tensor_scalar(w_mean[0:EA, 1:2], w_mean[0:EA, 0:1], 1.0 / D, None, ALU.mult).then_inc(set_dve, 1)
            dve.wait_ge(set_dve, 3)
            nc.vector.tensor_scalar(wc[0:EA, :], w_emb[0:EA, :], w_mean[0:EA, 1:2], None, ALU.subtract).then_inc(set_dve, 1)
            dve.wait_ge(set_act, 4)
            nc.vector.scalar_tensor_tensor(out=m_l[0:EA, 0:D], in0=ps_vec[0:EA, 0, :], scalar=QSCALE,
                                           in1=m_h[0:EA, 0:D].bitcast(F32), op0=ALU.mult, op1=ALU.subtract).then_inc(set_dve, 1)
            nc.vector.tensor_tensor(m_l[0:EA, D:QKV], ps_vec[0:EA, 1, 0:QKV - D], m_h[0:EA, D:QKV].bitcast(F32),
                                    ALU.subtract).then_inc(set_dve, 1)

            e_lo(0)
            norm_stats(0)
            e_scale(0)
            e2_lo(0)
            qk_lo(0)
            for c in range(KV):
                maxima(0, c)
            for i, (_, hi, lo) in enumerate(pieces):
                dve.wait_ge(part_hi, i + 1)
                nc.vector.tensor_tensor(lo, stage[:, i % 2, :], hi.bitcast(F32), ALU.subtract).then_inc(part_lo, 1)
            m_lo(0)
            for c in range(KV):
                normalise(0, c)
            for t in range(TT):
                residual(0, t)
            for t in range(TT):
                norm_x(0, t)
            iteration(1, 0)
            with dve.Fori(2, NB) as b:
                iteration(b, b - 1)
            iteration(None, NB - 1)

        @block.tensor
        def _(pe):
            def passes(dst, chunks):
                n = 3 * len(chunks)
                i = 0
                for l_h, l_l, r_h, r_l in chunks:
                    for lhs, rhs in ((l_h, r_h), (l_h, r_l), (l_l, r_h)):
                        mm = nc.tensor.matmul(dst, lhs, rhs, start=(i == 0), stop=(i == n - 1))
                        i += 1
                return mm

            def e_turn(b):
                after(pe, gathered, b, 16 * TT, 16 * TT)
                after(pe, exp_ready, b - 1, 2 * KV, 2 * KV)
                for t in range(TT):
                    mm = nc.tensor.transpose(ps_small[0:EA, t * P:(t + 1) * P], e_tok[:, t, :], ident[:, :])
                mm.then_inc(et_done, 1)

            def h0_product(b):
                after(pe, etl_ready, b, 1, 1)
                for t in range(TT):
                    tok = slice(t * P, (t + 1) * P)
                    passes(ps_pair[:, t, :], [(et_h[:, tok], et_l[:, tok], we_h[:, :], we_l[:, :])]).then_inc(h0_done, 1)

            def e2_turn(b):
                after(pe, e2_ready, b, TT, TT)
                for t in range(TT):
                    mm = nc.tensor.transpose(ps_small[0:EA, t * P:(t + 1) * P], e_scaled[:, t, :], ident[:, :])
                mm.then_inc(e2t_done, 1)

            def qkv_product(b):
                after(pe, e2l_ready, b, 1, 1)
                cols = slice(D, D + KD)
                passes(ps_small[:, 0:S], [(m_h[:, cols], m_l[:, cols], e2_h[:, :], e2_l[:, :])]).then_inc(k_done, 1)
                after(pe, h0_ready, b, TT, TT)
                for c in range(KV):
                    cols = slice(c * P, (c + 1) * P)
                    mm = passes(ps_pair[:, c // 2, (c % 2) * S:(c % 2 + 1) * S],
                                [(m_h[:, cols], m_l[:, cols], e2_h[:, :], e2_l[:, :])])
                    if c % 2:
                        mm.then_inc(q_done, 1)
                after(pe, o_ready, b - 1, KV, KV)
                for t in range(TT):
                    tok = slice(t * P, (t + 1) * P)
                    mm = passes(ps_od[:, t * 2 * KD:(t + 1) * 2 * KD],
                                [(e2_h[:, tok], e2_l[:, tok], m_h[:, D:QKV], m_l[:, D:QKV])])
                mm.then_inc(v_done, 1)

            def scores(b, c):
                for g in range(GROUP):
                    n = GROUP * c + g
                    if n == 0:
                        after(pe, stacked, b, n_stack, n_stack)
                    if n < 2:
                        after(pe, ql_ready, b, 2, n + 1)
                    else:
                        after(pe, max_ready, b, HEADS, n - 1)
                    for t in range(TT):
                        mm = nc.tensor.matmul(ps_pair[:, n % 2, t * S:(t + 1) * S],
                                              q_stack[0:QSTACK, g, c, t * P:(t + 1) * P], k_stack[0:QSTACK, c, :],
                                              start=True, stop=True)
                    mm.then_inc(s_done, 1)

            def max_turn(b):
                after(pe, max_ready, b, HEADS, HEADS)
                after(pe, kl_ready, b, 1, 1)
                nc.tensor.transpose(ps_small[0:TT * HEADS, 0:P], row_max[:, :, :].rearrange("p t h -> p (t h)"),
                                    ident[:, :]).then_inc(mt_done, 1)

            def scores_t(b, c):
                if c == 0:
                    after(pe, m_stacked, b, n_mrow, n_mrow)
                else:
                    after(pe, exp_ready, b, 2 * KV, 2 * c)
                for i in range(2):
                    nc.tensor.matmul(ps_pair[:, i, :], k_stack[0:STACK, c, 0:P], q_stack[0:STACK, 2 * i:2 * i + 2, c, :],
                                     start=True, stop=True)
                    nc.tensor.matmul(ps_pair[:, i, :].rearrange("p (g q) -> p g q", g=2)[:, :, 0:P], ident_b[:, :],
                                     mask_t[:, :].unsqueeze(1).broadcast_to([P, 2, P]), start=False, stop=True,
                                     skip_group_check=True)
                nc.tensor.matmul(ps_small[:, :], k_stack[0:STACK, c, P:S], q_stack[0:STACK, :, c, P:S],
                                 start=True, stop=False)
                nc.tensor.matmul(ps_small[:, :], ident_b[:, :], mask_t[:, :].unsqueeze(1).broadcast_to([P, GROUP, P]),
                                 start=False, stop=True).then_inc(st_done, 1)

            def values(b, c):
                after(pe, exp_ready, b, 2 * KV, 2 * c + 2)
                if c == 0:
                    after(pe, v_ready, b, 1, 1)
                else:
                    after(pe, o_ready, b, KV, c)
                for what in range(2):
                    for t in range(TT):
                        for g in range(GROUP):
                            rows = slice(HD * g, HD * (g + 1))
                            lhs = v_tok[:, t, HD * c:HD * (c + 1)] if what == 0 else ones[:, :]
                            rhs = prob0[:, c % 2, g, :] if t == 0 else prob1[:, c % 2, g, :]
                            mm = nc.tensor.matmul(ps_od[rows, what * S + t * P:(what + 1) * S], lhs, rhs,
                                                  start=(t == 0), stop=(t == 1), tile_position=(0, HD * g))
                mm.then_inc(pv_done, 1)

            def out_product(b, t):
                if t == 0:
                    after(pe, otl_ready, b, KV, KV)
                    after(pe, result_ready, b - 1, TT, TT)
                else:
                    after(pe, h1_ready, b, TT, 1)
                tok = slice(t * P, (t + 1) * P)
                passes(ps_acc[:, :], [(ot_h[:, c, tok], ot_l[:, c, tok], wo_h[:, c * D:(c + 1) * D],
                                       wo_l[:, c * D:(c + 1) * D]) for c in range(DC)]).then_inc(wo_done, 1)

            def x_turn(f, t):
                after(pe, x_ready, f, TT, t + 1)
                if t == 0:
                    after(pe, utl_ready, f - 1, 2 * TT, 2 * TT)
                else:
                    after(pe, xl_ready, f, TT, 1)
                for c in range(DC):
                    mm = nc.tensor.transpose(ps_turn[:, c * P:(c + 1) * P], x[:, t, c * P:(c + 1) * P], ident[:, :])
                mm.then_inc(xt_done, 1)

            def vec_product(f, t):
                after(pe, xl_ready, f, TT, t + 1)
                after(pe, routed_ready, f, TT, t)
                for n in range(2):
                    passes(ps_vec[:, n, :], [(xt_h[:, t, c, :], xt_l[:, t, c, :],
                                              at_h[:, c * AR + n * 512:c * AR + (n + 1) * 512],
                                              at_l[:, c * AR + n * 512:c * AR + (n + 1) * 512])
                                             for c in range(DC)]).then_inc(vec_done, 1)

            def base_product(f, t):
                if t == 0:
                    after(pe, h1_ready, f, TT, TT)
                else:
                    after(pe, result_ready, f, TT, 1)
                i = 0
                for c in range(DC):
                    w = slice(c * D, (c + 1) * D)
                    for lhs, rhs in ((xt_h, wt_h), (xt_h, wt_l), (xt_l, wt_h)):
                        nc.tensor.matmul(ps_acc[:, :], lhs[:, t, c, :], rhs[:, w], start=(i == 0), stop=False)
                        i += 1

            def u_turn(f, t, h):
                if h == 0:
                    after(pe, u_ready, f, TT, t + 1)
                    if t == 0:
                        after(pe, xl_ready, f, TT, TT)
                after(pe, utl_ready, f, 2 * TT, 2 * t + h)
                for i in range(4):
                    k = 4 * h + i
                    mm = nc.tensor.transpose(ps_turn[:, i * P:(i + 1) * P], u[:, k * P:(k + 1) * P], ident[:, :])
                mm.then_inc(ut_done, 1)

            def delta_product(f, t, h):
                after(pe, utl_ready, f, 2 * TT, 2 * t + h + 1)
                for k in range(4 * h, 4 * h + 4):
                    w = slice(k * D, (k + 1) * D)
                    for j, (lhs, rhs) in enumerate(((ut_h, bt_h), (ut_h, bt_l), (ut_l, bt_h))):
                        mm = nc.tensor.matmul(ps_acc[:, :], lhs[:, k, :], rhs[:, w], start=False,
                                              stop=(k == RC - 1 and j == 2))
                if h == 1:
                    mm.then_inc(acc_done, 1)

            def iteration(b, f):
                if b is not None:
                    e_turn(b)
                if f is not None:
                    x_turn(f, 0)
                if b is not None:
                    h0_product(b)
                if f is not None:
                    vec_product(f, 0)
                    x_turn(f, 1)
                if b is not None:
                    e2_turn(b)
                if f is not None:
                    base_product(f, 0)
                if b is not None:
                    qkv_product(b)
                if f is not None:
                    vec_product(f, 1)
                    u_turn(f, 0, 0)
                if b is not None:
                    scores(b, 0)
                if f is not None:
                    u_turn(f, 0, 1)
                    delta_product(f, 0, 0)
                if b is not None:
                    scores(b, 1)
                    scores(b, 2)
                if f is not None:
                    delta_product(f, 0, 1)
                if b is not None:
                    scores(b, 3)
                    max_turn(b)
                if f is not None:
                    base_product(f, 1)
                if b is not None:
                    scores_t(b, 0)
                if f is not None:
                    u_turn(f, 1, 0)
                if b is not None:
                    scores_t(b, 1)
                    values(b, 0)
                if f is not None:
                    u_turn(f, 1, 1)
                    delta_product(f, 1, 0)
                if b is not None:
                    scores_t(b, 2)
                    values(b, 1)
                if f is not None:
                    delta_product(f, 1, 1)
                if b is not None:
                    scores_t(b, 3)
                    values(b, 2)
                    values(b, 3)
                    for t in range(TT):
                        out_product(b, t)

            pe.wait_ge(const_pool, 11)
            pe.wait_ge(const_dve, 1)
            pe.wait_ge(set_dve, 4)
            for c in range(DC):
                mm = nc.tensor.transpose(ps_turn[:, c * P:c * P + EA], wc[0:EA, c * P:(c + 1) * P], ident[0:EA, 0:EA])
            mm.then_inc(set_pe, 1)
            pe.wait_ge(set_act, 2)
            pe.wait_ge(qkv_in, 48)
            for n, (lo, hi) in enumerate(((0, D), (D, QKV))):
                for c in range(DC):
                    mm = nc.tensor.matmul(ps_vec[0:EA, n, 0:hi - lo], wc_t[:, c, 0:EA], w_qkv[:, c, lo:hi],
                                          start=(c == 0), stop=(c == DC - 1))
            mm.then_inc(set_pe, 1)
            pe.wait_ge(set_dve, 6)
            e_turn(0)
            h0_product(0)
            e2_turn(0)
            qkv_product(0)
            for c in range(KV):
                scores(0, c)
            max_turn(0)
            for c in range(KV):
                scores_t(0, c)
                if c:
                    values(0, c - 1)
            values(0, KV - 1)
            pe.wait_ge(part_lo, len(pieces))
            for t in range(TT):
                out_product(0, t)
            iteration(1, 0)
            with pe.Fori(2, NB) as b:
                iteration(b, b - 1)
            iteration(None, NB - 1)


def kernel(x, L0_tok_emb, L0_tok_W, L0_tok_b, L0_attn_Wq, L0_attn_Wk, L0_attn_Wv, L0_attn_Wo,
           L0_ffn_A, L0_ffn_B, L0_ffn_W, L0_ffn_bias):
    import numpy as np
    import concourse.bacc as bacc
    from concourse.bass_utils import run_bass_kernel_spmd

    x = np.asarray(x)
    A = np.asarray(L0_ffn_A)
    B = np.asarray(L0_ffn_B)
    arrays = {
        "ids": np.ascontiguousarray(x.reshape(-1, 128).T),
        "emb": np.ascontiguousarray(L0_tok_emb),
        "w_tok": np.ascontiguousarray(L0_tok_W),
        "b_tok": np.ascontiguousarray(L0_tok_b),
        "w_q": np.ascontiguousarray(L0_attn_Wq),
        "w_k": np.ascontiguousarray(L0_attn_Wk),
        "w_v": np.ascontiguousarray(L0_attn_Wv),
        "w_o": np.ascontiguousarray(L0_attn_Wo),
        "a_t": np.ascontiguousarray(A.reshape(-1, A.shape[2]).T),
        "b_t": np.ascontiguousarray(B.transpose(0, 2, 1).reshape(-1, B.shape[1])),
        "w_t": np.ascontiguousarray(np.asarray(L0_ffn_W).T),
        "bias": np.ascontiguousarray(L0_ffn_bias),
    }
    nc = bacc.Bacc("TRN2", target_bir_lowering=False, num_devices=1)
    args = [nc.dram_tensor(n, a.shape, mybir.dt.from_np(a.dtype), kind="ExternalInput").ap() for n, a in arrays.items()]
    out = nc.dram_tensor("out", (x.size, L0_tok_W.shape[1]), F32, kind="ExternalOutput").ap()
    tower_kernel(nc, *args, out)
    r = run_bass_kernel_spmd(nc, [arrays], core_ids=[0])
    return r.results[0]["out"].reshape(*x.shape, -1)
```

```python
from contextlib import ExitStack

import concourse.bass as bass
from concourse import mybir

F32 = mybir.dt.float32
F32R = mybir.dt.float32r
BF16 = mybir.dt.bfloat16
I32 = mybir.dt.int32
U32 = mybir.dt.uint32
ALU = mybir.AluOpType
ACT = mybir.ActivationFunctionType
AX = mybir.AxisListType

P = 128
HEADS = 16
KV = 4
GROUP = HEADS // KV
TOPK = 4
EPS = 1e-5
NEVER = -1e30
HUGE = 3e38


def tower_kernel(nc, ids, emb, w_tok, b_tok, w_q, w_k, w_v, w_o, a_t, b_t, w_t, bias, out):
    EMB = emb.shape[1]
    EA = EMB + 1
    D = w_tok.shape[1]
    DC = D // P
    NT = ids.shape[1]
    TT = 2
    S = TT * P
    NB = NT // TT
    HD = D // HEADS
    KD = KV * HD
    QKV = D + 2 * KD
    AR = a_t.shape[1]
    NA = AR // 16
    R = AR // NA
    RC = AR // P
    ROOT = float(D) ** 0.5
    QSCALE = float(HD) ** -0.5
    assert HD == 32 and KD == P and S == 256 and D == 512 and AR == 1024 and RC == 8
    QSTACK = 3 * HD
    STACK = QSTACK + 2

    with ExitStack() as ctx:
        def sb(name, shape, dt=F32):
            return ctx.enter_context(nc.sbuf_tensor(name, shape, dt))

        def psum(name, shape, dt=F32):
            return ctx.enter_context(nc.psum_tensor(name, shape, dt))

        def sem(name):
            return ctx.enter_context(nc.semaphore(name))

        ps_pair = psum("ps_pair", [P, 2, 512])
        ps_small = psum("ps_small", [P, 512])
        ps_od = psum("ps_od", [P, 512])
        ps_vec = psum("ps_vec", [P, 2, 512])
        ps_acc = psum("ps_acc", [P, 512])
        ps_turn = psum("ps_turn", [P, 512])

        ident = sb("ident", [P, P])
        mask = sb("mask", [P, S])
        ident_b = sb("ident_b", [P, P], BF16)
        mask_t = sb("mask_t", [P, P], BF16)
        ones = mask[:, 0:HD]
        minus_half = sb("minus_half", [P, TT])
        bias_rows = sb("bias_rows", [P, D])
        idx_all = sb("idx_all", [P, NT + TT], I32)
        idx_now = sb("idx_now", [P, TT], I32)

        shared_a = sb("shared_a", [P, 8 * D])
        stage = shared_a[:, :].rearrange("p (i n) -> p i n", i=2)
        squares = shared_a[:, 0:AR]
        routed = squares
        u = shared_a[:, AR:2 * AR]
        result = shared_a[:, 4 * D:6 * D].rearrange("p (t n) -> p t n", t=TT)
        x = shared_a[:, 6 * D:8 * D].rearrange("p (t n) -> p t n", t=TT)
        shared_b = sb("shared_b", [P, 6 * D])
        w_qkv = shared_b[:, :].rearrange("p (c n) -> p c n", c=DC)
        h0 = shared_b[:, 0:TT * D].rearrange("p (t n) -> p t n", t=TT)
        h1 = shared_b[:, TT * D:2 * TT * D].rearrange("p (t n) -> p t n", t=TT)
        h0_next = shared_b[:, 2 * TT * D:3 * TT * D].rearrange("p (t n) -> p t n", t=TT)
        prob0 = sb("prob0", [P, 2, GROUP, S])
        prob1 = sb("prob1", [P, 2, GROUP, P])
        w_emb = prob1[:, 0, :, :].rearrange("p g s -> p (g s)")
        wc = prob0[:, 0, :, :].rearrange("p g s -> p (g s)")[:, 0:D]
        wc_t = prob0[:, 1, :, :].rearrange("p g s -> p (g s)")[:, 0:D].rearrange("p (c n) -> p c n", c=DC)
        w_mean = sb("w_mean", [P, 2])
        we_h = sb("we_h", [P, D], F32R)
        we_l = sb("we_l", [P, D], F32R)
        m_h = sb("m_h", [P, QKV], F32R)
        m_l = sb("m_l", [P, QKV], F32R)
        wo_h = sb("wo_h", [P, DC * D], F32R)
        wo_l = sb("wo_l", [P, DC * D], F32R)
        at_h = sb("at_h", [P, DC * AR], F32R)
        at_l = sb("at_l", [P, DC * AR], F32R)
        wt_h = sb("wt_h", [P, DC * D], F32R)
        wt_l = sb("wt_l", [P, DC * D], F32R)
        bt_h = sb("bt_h", [P, RC * D], F32R)
        bt_l = sb("bt_l", [P, RC * D], F32R)

        e_tok = sb("e_tok", [P, TT, EA])
        e_scaled = sb("e_scaled", [P, TT, EA])
        et_h = sb("et_h", [P, S], F32R)
        et_l = sb("et_l", [P, S], F32R)
        e2_h = sb("e2_h", [P, S], F32R)
        e2_l = sb("e2_l", [P, S], F32R)
        stats = sb("stats", [P, TT, 6])
        mean_var = sb("mean_var", [P, TT, 2])
        var_eps = sb("var_eps", [P, TT])
        rstd = sb("rstd", [P, TT])
        q_h = sb("q_h", [P, KV, S], F32R)
        q_l = sb("q_l", [P, KV, S], F32R)
        k_h = sb("k_h", [P, S], F32R)
        k_l = sb("k_l", [P, S], F32R)
        q_stack = sb("q_stack", [P, GROUP, KV, S], F32R)
        k_stack = sb("k_stack", [P, KV, S], F32R)
        v_tok = sb("v_tok", [P, TT, KD])
        row_max = sb("row_max", [P, TT, HEADS])
        m_rows_h = sb("m_rows_h", [TT * HEADS, P], F32R)
        m_rows_l = sb("m_rows_l", [TT * HEADS, P], F32R)
        rden = sb("rden", [P, S])
        o_t = sb("o_t", [P, 2, S])
        ot_h, ot_l = q_h, q_l

        stats2 = sb("stats2", [P, TT, 6])
        mean_var2 = sb("mean_var2", [P, TT, 2])
        var_eps2 = sb("var_eps2", [P, TT])
        rstd2 = sb("rstd2", [P, TT])
        xt_h = sb("xt_h", [P, TT, DC, P], F32R)
        xt_l = sb("xt_l", [P, TT, DC, P], F32R)
        arrows = sb("arrows", [P, NA + TOPK])
        top8 = sb("top8", [P, 8])
        struck = sb("struck", [P, NA + TOPK])
        route = sb("route", [P, NA])
        v_sum = sb("v_sum", [P, R])
        ut_h = sb("ut_h", [P, RC, P], F32R)
        ut_l = sb("ut_l", [P, RC, P], F32R)

        passed = sem("passed")
        const_pool = sem("const_pool")
        const_dve = sem("const_dve")
        idx_in = sem("idx_in")
        small_in = sem("small_in")
        qkv_in = sem("qkv_in")
        bias_in = sem("bias_in")
        big_in = [sem("big_in0"), sem("big_in1")]
        set_dve = sem("set_dve")
        set_act = sem("set_act")
        set_pe = sem("set_pe")
        part_hi = sem("part_hi")
        part_lo = sem("part_lo")

        idx_ready = sem("idx_ready")
        gathered = sem("gathered")
        et_done = sem("et_done")
        eth_ready = sem("eth_ready")
        etl_ready = sem("etl_ready")
        h0_done = sem("h0_done")
        h0_ready = sem("h0_ready")
        h0_moved = sem("h0_moved")
        dve_attn = sem("dve_attn")
        mv_ready = sem("mv_ready")
        eps_ready = sem("eps_ready")
        rstd_ready = sem("rstd_ready")
        e2_ready = sem("e2_ready")
        e2t_done = sem("e2t_done")
        e2h_ready = sem("e2h_ready")
        e2l_ready = sem("e2l_ready")
        k_done = sem("k_done")
        q_done = sem("q_done")
        v_done = sem("v_done")
        kh_ready = sem("kh_ready")
        kl_ready = sem("kl_ready")
        qh_ready = sem("qh_ready")
        ql_ready = sem("ql_ready")
        v_ready = sem("v_ready")
        k_stacked = sem("k_stacked")
        q_stacked = [sem(f"q_stacked{g}") for g in range(GROUP)]
        s_done = sem("s_done")
        max_ready = sem("max_ready")
        mt_done = sem("mt_done")
        mh_ready = sem("mh_ready")
        ml_ready = sem("ml_ready")
        m_stacked = sem("m_stacked")
        st_done = sem("st_done")
        exp_ready = sem("exp_ready")
        pv_done = sem("pv_done")
        rden_ready = sem("rden_ready")
        o_ready = sem("o_ready")
        oth_ready = sem("oth_ready")
        otl_ready = sem("otl_ready")
        wo_done = sem("wo_done")
        h1_ready = sem("h1_ready")
        stats2_ready = sem("stats2_ready")
        mv2_ready = sem("mv2_ready")
        eps2_ready = sem("eps2_ready")
        rstd2_ready = sem("rstd2_ready")
        x_ready = sem("x_ready")
        hb_ready = sem("hb_ready")

        xt_done = sem("xt_done")
        xh_ready = sem("xh_ready")
        xl_ready = sem("xl_ready")
        vec_done = sem("vec_done")
        sq_ready = sem("sq_ready")
        dve_route = sem("dve_route")
        route_ready = sem("route_ready")
        routed_ready = sem("routed_ready")
        vsum_ready = sem("vsum_ready")
        u_ready = sem("u_ready")
        ut_done = sem("ut_done")
        uth_ready = sem("uth_ready")
        utl_ready = sem("utl_ready")
        acc_done = sem("acc_done")
        result_ready = sem("result_ready")
        stored = [sem("stored0"), sem("stored1")]

        def after(eng, s, b, per, k):
            n = b * per + k
            if isinstance(n, int) and n <= 0:
                return
            eng.wait_ge(s, n)

        def after_apart(eng, s, b, per, k):
            after(eng, s, b, per, k)
            if not isinstance(b, int):
                eng.sem_inc(passed, 1)

        n_kstack = 3 * KV * 16
        n_qstack = 3 * 16
        n_mrow = 2 * TT * 16

        pieces = []
        for weight, hi, lo, n in ((w_o, wo_h, wo_l, 1), (a_t, at_h, at_l, 2), (w_t, wt_h, wt_l, 1), (b_t, bt_h, bt_l, 2)):
            src = weight.rearrange("(c p) n -> p c n", p=P)
            c = src.shape[1] // n
            for i in range(n):
                w = 4 * D
                pieces.append((src[:, i * c:(i + 1) * c, :], hi[:, i * w:(i + 1) * w], lo[:, i * w:(i + 1) * w]))

        block = ctx.enter_context(nc.Block())

        @block.sync
        def _(sp):
            sp.dma_start(idx_all[:, 0:NT], ids).then_inc(idx_in, 16)
            sp.dma_start(w_emb[0:EMB, :], w_tok).then_inc(small_in, 16)
            sp.dma_start(w_emb[EMB:EA, :], b_tok.rearrange("(o n) -> o n", o=1)).then_inc(small_in, 16)
            sp.dma_start(w_qkv[:, :, 0:D], w_q.rearrange("(c p) n -> p c n", p=P)).then_inc(qkv_in, 16)
            sp.dma_start(w_qkv[:, :, D:D + KD], w_k.rearrange("(c p) n -> p c n", p=P)).then_inc(qkv_in, 16)
            sp.dma_start(w_qkv[:, :, D + KD:QKV], w_v.rearrange("(c p) n -> p c n", p=P)).then_inc(qkv_in, 16)
            sp.dma_start(bias_rows[:, :], bias.rearrange("(o n) -> o n", o=1).broadcast_to([P, D])).then_inc(bias_in, 16)

            def load_piece(i):
                if i >= 2:
                    sp.wait_ge(part_lo, i - 1)
                src = pieces[i][0]
                dst = stage[:, i % 2, :].rearrange("p (c n) -> p c n", n=src.shape[2])
                sp.dma_start(dst, src).then_inc(big_in[i % 2], 16)

            load_piece(0)
            load_piece(1)

            def stack_k(b):
                after_apart(sp, st_done, b - 1, 3 * KV, 3 * KV)
                after_apart(sp, kl_ready, b, 1, 1)
                for c in range(KV):
                    rows = slice(HD * c, HD * (c + 1))
                    for slot, part in ((0, k_h), (1, k_l), (2, k_h)):
                        sp.dma_start(k_stack[HD * slot:HD * (slot + 1), c, :].bitcast(F32),
                                     part[rows, :].bitcast(F32)).then_inc(k_stacked, 16)

            def stack_q(b):
                after_apart(sp, ql_ready, b, 2, 2)
                for g in range(GROUP):
                    rows = slice(HD * g, HD * (g + 1))
                    for slot, part in ((0, q_h), (1, q_h), (2, q_l)):
                        sp.dma_start(q_stack[HD * slot:HD * (slot + 1), g, :, :].bitcast(F32),
                                     part[rows, :, :].bitcast(F32)).then_inc(q_stacked[g], 16)

            def stack_max(b):
                after_apart(sp, ml_ready, b, 1, 1)
                for slot, part in enumerate((m_rows_h, m_rows_l)):
                    for t in range(TT):
                        row = q_stack[QSTACK + slot:QSTACK + slot + 1, :, :, t * P:(t + 1) * P]
                        sp.dma_start(row.rearrange("o g c q -> o (g c) q").bitcast(F32),
                                     part[HEADS * t:HEADS * (t + 1), :].bitcast(F32)).then_inc(m_stacked, 16)

            def store(f, t):
                after_apart(sp, result_ready, f, TT, t + 1)
                sp.dma_start(out[bass.ds(f * S + t * P, P), :], result[:, t, :]).then_inc(stored[t], 16)

            def iteration(b, f, n):
                if f is not None:
                    store(f, 0)
                if b is not None:
                    stack_max(b)
                if n is not None:
                    stack_k(n)
                if f is not None:
                    store(f, 1)
                if n is not None:
                    stack_q(n)

            stack_k(0)
            stack_q(0)
            for i in range(2, len(pieces)):
                load_piece(i)
            iteration(0, None, 1)
            iteration(1, 0, 2)
            with sp.Fori(2, NB - 1) as b:
                iteration(b, b - 1, b + 1)
            iteration(NB - 1, NB - 2, None)
            iteration(None, NB - 1, None)
            for t in range(TT):
                sp.wait_ge(stored[t], 16 * NB)

        @block.gpsimd
        def _(pool):
            nc.gpsimd.memset(ident[:, :], 0.0).then_inc(const_pool, 1)
            nc.gpsimd.memset(mask[:, :], 1.0).then_inc(const_pool, 1)
            nc.gpsimd.memset(minus_half[:, :], -0.5).then_inc(const_pool, 1)
            nc.gpsimd.memset(idx_all[:, NT:NT + TT], 0).then_inc(const_pool, 1)
            nc.gpsimd.memset(e_tok[:, :, EMB:EA], 1.0).then_inc(const_pool, 1)
            nc.gpsimd.memset(ident_b[:, :], 0.0).then_inc(const_pool, 1)
            nc.gpsimd.memset(mask_t[:, :], 0.0).then_inc(const_pool, 1)
            pool.wait_ge(const_pool, 7)
            nc.gpsimd.affine_select(out=ident_b[:, :], in_=ident_b[:, :], compare_op=ALU.not_equal, fill=1.0,
                                    base=0, pattern=[[-1, P]], channel_multiplier=1).then_inc(const_pool, 1)
            nc.gpsimd.affine_select(out=mask_t[:, :], in_=mask_t[:, :], compare_op=ALU.is_ge, fill=NEVER,
                                    base=0, pattern=[[1, P]], channel_multiplier=-1).then_inc(const_pool, 1)
            nc.gpsimd.affine_select(out=ident[:, :], in_=ident[:, :], compare_op=ALU.not_equal, fill=1.0,
                                    base=0, pattern=[[-1, P]], channel_multiplier=1).then_inc(const_pool, 1)
            nc.gpsimd.affine_select(out=mask[:, P:S], in_=mask[:, P:S], compare_op=ALU.is_ge, fill=NEVER,
                                    base=0, pattern=[[-1, P]], channel_multiplier=1).then_inc(const_pool, 1)

            def gather(b):
                after(pool, e2_ready, b - 1, TT, TT)
                after(pool, gathered, b - 1, 16 * TT, 16 * TT)
                nc.gpsimd.tensor_copy(idx_now[:, :], idx_all[:, bass.ds(b * TT, TT)]).then_inc(idx_ready, 1)
                after_apart(pool, idx_ready, b, 1, 1)
                for t in range(TT):
                    nc.gpsimd.indirect_dma_start(
                        out=e_tok[:, t, 0:EMB], out_offset=None, in_=emb,
                        in_offset=bass.IndirectOffsetOnAxis(ap=idx_now[:, t:t + 1].bitcast(U32), axis=0),
                    ).then_inc(gathered, 16)

            def rstd_attn(b):
                after_apart(pool, mv_ready, b, TT, TT)
                nc.gpsimd.tensor_scalar_add(var_eps[:, :], mean_var[:, :, 1], EPS).then_inc(eps_ready, 1)
                after(pool, eps_ready, b, 1, 1)
                nc.gpsimd.tensor_tensor(rstd[:, :], var_eps[:, :], minus_half[:, :], ALU.pow).then_inc(rstd_ready, 1)

            def o_lo(b, c):
                after(pool, oth_ready, b, KV, c + 1)
                nc.gpsimd.tensor_tensor(ot_l[:, c, :], o_t[:, c % 2, :], ot_h[:, c, :].bitcast(F32),
                                        ALU.subtract).then_inc(otl_ready, 1)

            def rstd_ffn(b, t):
                after_apart(pool, mv2_ready, b, TT, t + 1)
                nc.gpsimd.tensor_scalar_add(var_eps2[:, t:t + 1], mean_var2[:, t, 1:2], EPS).then_inc(eps2_ready, 1)
                after(pool, eps2_ready, b, TT, t + 1)
                nc.gpsimd.tensor_tensor(rstd2[:, t:t + 1], var_eps2[:, t:t + 1], minus_half[:, 0:1],
                                        ALU.pow).then_inc(rstd2_ready, 1)

            def add_bias(b, t):
                after(pool, stored[t], b, 16, 0)
                nc.gpsimd.tensor_tensor(result[:, t, :], h1[:, t, :], bias_rows[:, :], ALU.add).then_inc(hb_ready, 1)

            def spread(f, t):
                after(pool, vsum_ready, f, TT, t + 1)
                after(pool, ut_done, f, 2 * TT, 2 * t)
                nc.gpsimd.tensor_tensor(u[:, :].rearrange("p (a r) -> p a r", r=R),
                                        route[:, :].unsqueeze(2).broadcast_to([P, NA, R]),
                                        v_sum[:, :].unsqueeze(1).broadcast_to([P, NA, R]),
                                        ALU.mult).then_inc(u_ready, 1)

            def iteration(b, f, n):
                if f is not None:
                    spread(f, 0)
                    spread(f, 1)
                if n is not None:
                    rstd_attn(n)
                    gather(n + 1)
                if b is not None:
                    for c in range(KV):
                        o_lo(b, c)
                    for t in range(TT):
                        rstd_ffn(b, t)
                    for t in range(TT):
                        add_bias(b, t)

            pool.wait_ge(idx_in, 16)
            pool.wait_ge(bias_in, 16)
            gather(0)
            rstd_attn(0)
            gather(1)
            iteration(0, None, 1)
            iteration(1, 0, 2)
            with pool.Fori(2, NB - 1) as b:
                iteration(b, b - 1, b + 1)
            iteration(NB - 1, NB - 2, None)
            iteration(None, NB - 1, None)
            pool.wait_ge(gathered, (NB + 1) * 16 * TT)

        @block.scalar
        def _(act):
            def e_hi(b):
                after(act, et_done, b, 1, 1)
                nc.scalar.copy(et_h[0:EA, :], ps_od[0:EA, 0:S]).then_inc(eth_ready, 1)

            def h0_out(b):
                after(act, h0_moved, b, TT, 0)
                for t in range(TT):
                    after(act, h0_done, b, TT, t + 1)
                    nc.scalar.mul(h0_next[:, t, :], ps_vec[:, t, :], ROOT).then_inc(h0_ready, 1)

            def h0_move(b):
                after(act, h0_ready, b, TT, TT)
                for t in range(TT):
                    after(act, h1_ready, b - 1, TT, t + 1)
                    nc.scalar.copy(h0[:, t, :], h0_next[:, t, :]).then_inc(h0_moved, 1)

            def e2_hi(b):
                after(act, e2t_done, b, 1, 1)
                nc.scalar.copy(e2_h[0:EA, :], ps_turn[0:EA, 0:S]).then_inc(e2h_ready, 1)

            def qkv_hi(b):
                after(act, k_stacked, b - 1, n_kstack, n_kstack)
                after(act, k_done, b, 1, 1)
                nc.scalar.copy(k_h[:, :], ps_small[:, 0:S]).then_inc(kh_ready, 1)
                after(act, wo_done, b - 1, TT, TT)
                for i in range(2):
                    after(act, q_done, b, 2, i + 1)
                    nc.scalar.copy(q_h[:, 2 * i:2 * i + 2, :].rearrange("p c s -> p (c s)"),
                                   ps_vec[:, i, :]).then_inc(qh_ready, 1)
                after(act, pv_done, b - 1, KV, KV)
                after(act, v_done, b, 1, 1)
                nc.scalar.copy(v_tok[:, :, :], ps_od[:, :].rearrange("p (t n) -> p t n", t=TT)[:, :, KD:2 * KD]).then_inc(v_ready, 1)

            def m_hi(b):
                after(act, mt_done, b, 1, 1)
                nc.scalar.mul(m_rows_h[:, :], ps_small[0:TT * HEADS, 0:P], -1.0).then_inc(mh_ready, 1)

            def exps(b, c):
                after(act, pv_done, b, KV, c - 1)
                for i in range(2):
                    after(act, st_done, b, 3 * KV, 3 * c + i + 1)
                    nc.scalar.activation(prob0[:, c % 2, 2 * i:2 * i + 2, :].rearrange("p g q -> p (g q)"),
                                         ps_pair[:, i, :], ACT.Exp, bias=ones[:, 0:1]).then_inc(exp_ready, 1)
                after(act, st_done, b, 3 * KV, 3 * c + 3)
                nc.scalar.activation(prob1[:, c % 2, :, :].rearrange("p g q -> p (g q)"), ps_small[:, :], ACT.Exp,
                                     bias=ones[:, 0:1]).then_inc(exp_ready, 1)

            def o_hi(b, c):
                after(act, o_ready, b, KV, c + 1)
                nc.scalar.copy(ot_h[:, c, :], o_t[:, c % 2, :]).then_inc(oth_ready, 1)

            def x_hi(f, t):
                after(act, acc_done, f - 1, TT, t + 1)
                after(act, xt_done, f, TT, t + 1)
                nc.scalar.copy(xt_h[:, t, :, :].rearrange("p c s -> p (c s)"), ps_turn[:, :]).then_inc(xh_ready, 1)

            def square(f, t, n):
                if n == 0:
                    after(act, vsum_ready, f, TT, t)
                after(act, vec_done, f, 2 * TT, 2 * t + n + 1)
                nc.scalar.activation(squares[:, n * 512:(n + 1) * 512], ps_vec[:, n, :], ACT.Square).then_inc(sq_ready, 1)

            def ut_hi(f, t, h):
                if h == 0:
                    after(act, acc_done, f, TT, t)
                after(act, ut_done, f, 2 * TT, 2 * t + h + 1)
                nc.scalar.copy(ut_h[:, 4 * h:4 * h + 4, :].rearrange("p c s -> p (c s)"), ps_turn[:, :]).then_inc(uth_ready, 1)

            def iteration(b, f, n):
                if f is not None:
                    x_hi(f, 1)
                    square(f, 0, 0)
                    square(f, 0, 1)
                    square(f, 1, 0)
                    ut_hi(f, 0, 0)
                    square(f, 1, 1)
                    ut_hi(f, 0, 1)
                if n is not None:
                    e_hi(n)
                    h0_out(n)
                if b is not None:
                    m_hi(b)
                if f is not None:
                    ut_hi(f, 1, 0)
                    ut_hi(f, 1, 1)
                if b is not None:
                    exps(b, 0)
                    exps(b, 1)
                    o_hi(b, 0)
                if n is not None:
                    e2_hi(n)
                if b is not None:
                    exps(b, 2)
                    o_hi(b, 1)
                    exps(b, 3)
                    o_hi(b, 2)
                    o_hi(b, 3)
                if n is not None:
                    qkv_hi(n)
                if b is not None:
                    x_hi(b, 0)
                if n is not None:
                    h0_move(n)

            act.wait_ge(small_in, 32)
            act.wait_ge(const_dve, 1)
            nc.scalar.copy(we_h[0:EA, :], w_emb[0:EA, :]).then_inc(set_act, 1)
            act.wait_ge(set_pe, 1)
            nc.scalar.copy(wc_t[:, :, 0:EA], ps_turn[:, :].rearrange("p (c n) -> p c n", c=DC)[:, :, 0:EA]).then_inc(set_act, 1)
            act.wait_ge(set_pe, 2)
            nc.scalar.mul(m_h[0:EA, 0:D], ps_vec[0:EA, 0, :], QSCALE).then_inc(set_act, 1)
            nc.scalar.copy(m_h[0:EA, D:QKV], ps_vec[0:EA, 1, 0:QKV - D]).then_inc(set_act, 1)

            e_hi(0)
            h0_out(0)
            e2_hi(0)
            h0_move(0)
            qkv_hi(0)
            for i, (_, hi, _lo) in enumerate(pieces):
                act.wait_ge(big_in[i % 2], 16 * (i // 2 + 1))
                nc.scalar.copy(hi, stage[:, i % 2, :]).then_inc(part_hi, 1)
            iteration(0, None, 1)
            iteration(1, 0, 2)
            with act.Fori(2, NB - 1) as b:
                iteration(b, b - 1, b + 1)
            iteration(NB - 1, NB - 2, None)
            iteration(None, NB - 1, None)

        @block.vector
        def _(dve):
            def e_lo(b):
                after(dve, eth_ready, b, 1, 1)
                nc.vector.tensor_tensor(et_l[0:EA, :], ps_od[0:EA, 0:S], et_h[0:EA, :].bitcast(F32),
                                        ALU.subtract).then_inc(etl_ready, 1)

            def norm_stats(b):
                for t in range(TT):
                    after(dve, h0_ready, b, TT, t + 1)
                    nc.vector.bn_stats(stats[:, t, :], h0_next[:, t, :]).then_inc(dve_attn, 1)
                for t in range(TT):
                    after_apart(dve, dve_attn, b, TT, t + 1)
                    nc.vector.bn_aggr(mean_var[:, t, :], stats[:, t, :]).then_inc(mv_ready, 1)

            def e_scale(b):
                after(dve, rstd_ready, b, 1, 1)
                for t in range(TT):
                    nc.vector.tensor_scalar(e_scaled[:, t, :], e_tok[:, t, :], rstd[:, t:t + 1], ROOT,
                                            ALU.mult, ALU.mult).then_inc(e2_ready, 1)

            def e2_lo(b):
                after(dve, e2h_ready, b, 1, 1)
                nc.vector.tensor_tensor(e2_l[0:EA, :], ps_turn[0:EA, 0:S], e2_h[0:EA, :].bitcast(F32),
                                        ALU.subtract).then_inc(e2l_ready, 1)

            def qk_lo(b):
                after(dve, kh_ready, b, 1, 1)
                nc.vector.tensor_tensor(k_l[:, :], ps_small[:, 0:S], k_h[:, :].bitcast(F32),
                                        ALU.subtract).then_inc(kl_ready, 1)
                for i in range(2):
                    after(dve, qh_ready, b, 2, i + 1)
                    nc.vector.tensor_tensor(q_l[:, 2 * i:2 * i + 2, :].rearrange("p c s -> p (c s)"), ps_vec[:, i, :],
                                            q_h[:, 2 * i:2 * i + 2, :].rearrange("p c s -> p (c s)").bitcast(F32),
                                            ALU.subtract).then_inc(ql_ready, 1)

            def maximum(b, n):
                after_apart(dve, s_done, b, HEADS, n + 1)
                nc.vector.tensor_tensor_reduce(out=ps_pair[:, n % 2, 0:P], in0=ps_pair[:, n % 2, 0:P], in1=mask[:, P:S],
                                               scale=1.0, scalar=-HUGE, op0=ALU.add, op1=ALU.max,
                                               accum_out=row_max[:, 0, n:n + 1])
                nc.vector.tensor_tensor_reduce(out=ps_pair[:, n % 2, S:2 * S], in0=ps_pair[:, n % 2, S:2 * S], in1=mask[:, :],
                                               scale=1.0, scalar=-HUGE, op0=ALU.add, op1=ALU.max,
                                               accum_out=row_max[:, 1, n:n + 1]).then_inc(max_ready, 1)

            def m_lo(b):
                after(dve, mh_ready, b, 1, 1)
                nc.vector.scalar_tensor_tensor(out=m_rows_l[:, :], in0=ps_small[0:TT * HEADS, 0:P], scalar=-1.0,
                                               in1=m_rows_h[:, :].bitcast(F32), op0=ALU.mult,
                                               op1=ALU.subtract).then_inc(ml_ready, 1)

            def normalise(b, c):
                od = ps_vec[:, 0, :] if c % 2 else ps_od[:, :]
                after(dve, pv_done, b, KV, c + 1)
                after(dve, o_ready, b, KV, c)
                nc.vector.reciprocal(rden[:, :], od[:, S:2 * S]).then_inc(rden_ready, 1)
                after(dve, otl_ready, b, KV, c - 1)
                after(dve, rden_ready, b, KV, c + 1)
                nc.vector.tensor_tensor(o_t[:, c % 2, :], od[:, 0:S], rden[:, :], ALU.mult).then_inc(o_ready, 1)

            def residual(b, t):
                after(dve, hb_ready, b - 1, TT, t + 1)
                after(dve, h0_moved, b, TT, t + 1)
                after(dve, wo_done, b, TT, t + 1)
                nc.vector.tensor_tensor(h1[:, t, :], ps_pair[:, t, :], h0[:, t, :], ALU.add).then_inc(h1_ready, 1)
                after(dve, h1_ready, b, TT, t + 1)
                nc.vector.bn_stats(stats2[:, t, :], h1[:, t, :]).then_inc(stats2_ready, 1)
                after_apart(dve, stats2_ready, b, TT, t + 1)
                nc.vector.bn_aggr(mean_var2[:, t, :], stats2[:, t, :]).then_inc(mv2_ready, 1)

            def norm_x(b, t):
                after(dve, rstd2_ready, b, TT, t + 1)
                nc.vector.tensor_scalar(x[:, t, :], h1[:, t, :], mean_var2[:, t, 0:1], rstd2[:, t:t + 1],
                                        ALU.subtract, ALU.mult).then_inc(x_ready, 1)

            def x_lo(f, t):
                after(dve, xh_ready, f, TT, t + 1)
                nc.vector.tensor_tensor(xt_l[:, t, :, :].rearrange("p c s -> p (c s)"), ps_turn[:, :],
                                        xt_h[:, t, :, :].rearrange("p c s -> p (c s)").bitcast(F32),
                                        ALU.subtract).then_inc(xl_ready, 1)

            def routing(f, t):
                after(dve, sq_ready, f, 2 * TT, 2 * t + 2)
                nc.vector.tensor_reduce(out=arrows[:, 0:NA], in_=squares[:, :].rearrange("p (a r) -> p a r", r=R),
                                        axis=AX.X, op=ALU.add).then_inc(dve_route, 1)
                after_apart(dve, dve_route, f, 3 * TT, 3 * t + 1)
                nc.vector.max(out=top8[:, :], in_=arrows[:, :]).then_inc(dve_route, 1)
                after_apart(dve, dve_route, f, 3 * TT, 3 * t + 2)
                nc.vector.match_replace(out=struck[:, :], in_to_replace=top8[:, :], in_values=arrows[:, :],
                                        imm_value=-1.0).then_inc(dve_route, 1)
                after(dve, u_ready, f, TT, t)
                after(dve, dve_route, f, 3 * TT, 3 * t + 3)
                nc.vector.tensor_scalar(route[:, :], struck[:, 0:NA], -1.0, 1.0 / TOPK, ALU.is_equal,
                                        ALU.mult).then_inc(route_ready, 1)
                after(dve, route_ready, f, TT, t + 1)
                nc.vector.tensor_tensor(routed[:, :].rearrange("p (a r) -> p a r", r=R),
                                        ps_vec[:, :, :].rearrange("p i (a r) -> p (i a) r", r=R),
                                        route[:, :].unsqueeze(2).broadcast_to([P, NA, R]),
                                        ALU.mult).then_inc(routed_ready, 1)
                after(dve, routed_ready, f, TT, t + 1)
                nc.vector.tensor_reduce(out=v_sum[:, :], in_=routed[:, :].rearrange("p (a r) -> p r a", r=R),
                                        axis=AX.X, op=ALU.add).then_inc(vsum_ready, 1)

            def ut_lo(f, t, h):
                after(dve, uth_ready, f, 2 * TT, 2 * t + h + 1)
                nc.vector.tensor_tensor(ut_l[:, 4 * h:4 * h + 4, :].rearrange("p c s -> p (c s)"), ps_turn[:, :],
                                        ut_h[:, 4 * h:4 * h + 4, :].rearrange("p c s -> p (c s)").bitcast(F32),
                                        ALU.subtract).then_inc(utl_ready, 1)

            def finish(f, t):
                after(dve, hb_ready, f, TT, t + 1)
                after(dve, acc_done, f, TT, t + 1)
                nc.vector.tensor_tensor(result[:, t, :], ps_acc[:, :], result[:, t, :], ALU.add).then_inc(result_ready, 1)

            def iteration(b, f, n):
                if f is not None:
                    x_lo(f, 1)
                    routing(f, 0)
                if b is not None:
                    for i in range(4):
                        maximum(b, i)
                if f is not None:
                    ut_lo(f, 0, 0)
                if b is not None:
                    for i in range(4, 6):
                        maximum(b, i)
                if f is not None:
                    ut_lo(f, 0, 1)
                    routing(f, 1)
                    finish(f, 0)
                if n is not None:
                    e_lo(n)
                if b is not None:
                    for i in range(6, 12):
                        maximum(b, i)
                if n is not None:
                    norm_stats(n)
                if b is not None:
                    for i in range(12, HEADS):
                        maximum(b, i)
                    m_lo(b)
                if n is not None:
                    e_scale(n)
                if f is not None:
                    ut_lo(f, 1, 0)
                    ut_lo(f, 1, 1)
                if b is not None:
                    normalise(b, 0)
                if n is not None:
                    e2_lo(n)
                if b is not None:
                    for c in range(1, KV):
                        normalise(b, c)
                    for t in range(TT):
                        residual(b, t)
                        norm_x(b, t)
                if n is not None:
                    qk_lo(n)
                if b is not None:
                    x_lo(b, 0)
                if f is not None:
                    finish(f, 1)

            for m in (we_h, we_l, m_h, m_l, et_h, et_l, e2_h, e2_l):
                nc.vector.memset(m[64:P, :].bitcast(F32), 0.0)
            nc.vector.memset(arrows[:, NA:NA + TOPK], HUGE)
            nc.vector.memset(k_stack[QSTACK:P, :, :].bitcast(F32), 1.0).then_inc(const_dve, 1)
            dve.wait_ge(const_dve, 1)

            dve.wait_ge(set_act, 1)
            nc.vector.tensor_tensor(we_l[0:EA, :], w_emb[0:EA, :], we_h[0:EA, :].bitcast(F32), ALU.subtract).then_inc(set_dve, 1)
            nc.vector.tensor_reduce(out=w_mean[0:EA, 0:1], in_=w_emb[0:EA, :], axis=AX.X, op=ALU.add).then_inc(set_dve, 1)
            dve.wait_ge(set_dve, 2)
            nc.vector.tensor_scalar(w_mean[0:EA, 1:2], w_mean[0:EA, 0:1], 1.0 / D, None, ALU.mult).then_inc(set_dve, 1)
            dve.wait_ge(set_dve, 3)
            nc.vector.tensor_scalar(wc[0:EA, :], w_emb[0:EA, :], w_mean[0:EA, 1:2], None, ALU.subtract).then_inc(set_dve, 1)
            dve.wait_ge(set_act, 4)
            nc.vector.scalar_tensor_tensor(out=m_l[0:EA, 0:D], in0=ps_vec[0:EA, 0, :], scalar=QSCALE,
                                           in1=m_h[0:EA, 0:D].bitcast(F32), op0=ALU.mult, op1=ALU.subtract).then_inc(set_dve, 1)
            nc.vector.tensor_tensor(m_l[0:EA, D:QKV], ps_vec[0:EA, 1, 0:QKV - D], m_h[0:EA, D:QKV].bitcast(F32),
                                    ALU.subtract).then_inc(set_dve, 1)

            e_lo(0)
            norm_stats(0)
            e_scale(0)
            e2_lo(0)
            qk_lo(0)
            for i, (_, hi, lo) in enumerate(pieces):
                dve.wait_ge(part_hi, i + 1)
                nc.vector.tensor_tensor(lo, stage[:, i % 2, :], hi.bitcast(F32), ALU.subtract).then_inc(part_lo, 1)
            iteration(0, None, 1)
            iteration(1, 0, 2)
            with dve.Fori(2, NB - 1) as b:
                iteration(b, b - 1, b + 1)
            iteration(NB - 1, NB - 2, None)
            iteration(None, NB - 1, None)

        @block.tensor
        def _(pe):
            def passes(dst, chunks):
                n = 3 * len(chunks)
                i = 0
                for l_h, l_l, r_h, r_l in chunks:
                    for lhs, rhs in ((l_h, r_h), (l_h, r_l), (l_l, r_h)):
                        mm = nc.tensor.matmul(dst, lhs, rhs, start=(i == 0), stop=(i == n - 1))
                        i += 1
                return mm

            def e_turn(b):
                after(pe, gathered, b, 16 * TT, 16 * TT)
                after(pe, v_ready, b - 1, 1, 1)
                for t in range(TT):
                    mm = nc.tensor.transpose(ps_od[0:EA, t * P:(t + 1) * P], e_tok[:, t, :], ident[:, :])
                mm.then_inc(et_done, 1)

            def h0_product(b):
                after(pe, etl_ready, b, 1, 1)
                after(pe, routed_ready, b - 2, TT, TT)
                for t in range(TT):
                    tok = slice(t * P, (t + 1) * P)
                    passes(ps_vec[:, t, :], [(et_h[:, tok], et_l[:, tok], we_h[:, :], we_l[:, :])]).then_inc(h0_done, 1)

            def e2_turn(b):
                after(pe, e2_ready, b, TT, TT)
                after(pe, utl_ready, b - 2, 2 * TT, 2 * TT)
                for t in range(TT):
                    mm = nc.tensor.transpose(ps_turn[0:EA, t * P:(t + 1) * P], e_scaled[:, t, :], ident[:, :])
                mm.then_inc(e2t_done, 1)

            def qkv_product(b):
                after(pe, e2l_ready, b, 1, 1)
                after(pe, exp_ready, b - 1, 3 * KV, 3 * KV)
                cols = slice(D, D + KD)
                passes(ps_small[:, 0:S], [(m_h[:, cols], m_l[:, cols], e2_h[:, :], e2_l[:, :])]).then_inc(k_done, 1)
                after(pe, h0_ready, b, TT, TT)
                after(pe, o_ready, b - 1, KV, KV)
                for c in range(KV):
                    cols = slice(c * P, (c + 1) * P)
                    mm = passes(ps_vec[:, c // 2, (c % 2) * S:(c % 2 + 1) * S],
                                [(m_h[:, cols], m_l[:, cols], e2_h[:, :], e2_l[:, :])])
                    if c % 2:
                        mm.then_inc(q_done, 1)
                for t in range(TT):
                    tok = slice(t * P, (t + 1) * P)
                    mm = passes(ps_od[:, t * 2 * KD:(t + 1) * 2 * KD],
                                [(e2_h[:, tok], e2_l[:, tok], m_h[:, D:QKV], m_l[:, D:QKV])])
                mm.then_inc(v_done, 1)

            def score(b, n):
                g, c = divmod(n, KV)
                if n == 0:
                    after(pe, k_stacked, b, n_kstack, n_kstack)
                if c == 0:
                    after(pe, q_stacked[g], b, n_qstack, n_qstack)
                if n < 2:
                    after(pe, h1_ready, b - 1, TT, n + 1)
                else:
                    after(pe, max_ready, b, HEADS, n - 1)
                for t in range(TT):
                    mm = nc.tensor.matmul(ps_pair[:, n % 2, t * S:(t + 1) * S],
                                          q_stack[0:QSTACK, g, c, t * P:(t + 1) * P], k_stack[0:QSTACK, c, :],
                                          start=True, stop=True)
                mm.then_inc(s_done, 1)

            def max_turn(b):
                after(pe, max_ready, b, HEADS, HEADS)
                after(pe, kl_ready, b, 1, 1)
                nc.tensor.transpose(ps_small[0:TT * HEADS, 0:P], row_max[:, :, :].rearrange("p t h -> p (t h)"),
                                    ident[:, :]).then_inc(mt_done, 1)

            def scores_t(b, c):
                if c == 0:
                    after(pe, m_stacked, b, n_mrow, n_mrow)
                for i in range(2):
                    if c > 0:
                        after(pe, exp_ready, b, 3 * KV, 3 * (c - 1) + i + 1)
                    nc.tensor.matmul(ps_pair[:, i, :], k_stack[0:STACK, c, 0:P], q_stack[0:STACK, 2 * i:2 * i + 2, c, :],
                                     start=True, stop=True)
                    nc.tensor.matmul(ps_pair[:, i, :].rearrange("p (g q) -> p g q", g=2)[:, :, 0:P], ident_b[:, :],
                                     mask_t[:, :].unsqueeze(1).broadcast_to([P, 2, P]), start=False, stop=True,
                                     skip_group_check=True).then_inc(st_done, 1)
                if c > 0:
                    after(pe, exp_ready, b, 3 * KV, 3 * c)
                nc.tensor.matmul(ps_small[:, :], k_stack[0:STACK, c, P:S], q_stack[0:STACK, :, c, P:S],
                                 start=True, stop=False)
                nc.tensor.matmul(ps_small[:, :], ident_b[:, :], mask_t[:, :].unsqueeze(1).broadcast_to([P, GROUP, P]),
                                 start=False, stop=True).then_inc(st_done, 1)

            def values(b, n, c):
                after(pe, exp_ready, b, 3 * KV, 3 * c + 3)
                if c == 0:
                    after(pe, v_ready, b, 1, 1)
                    if n is not None:
                        after(pe, etl_ready, n, 1, 1)
                elif c == 1:
                    if n is not None:
                        after(pe, h0_ready, n, TT, TT)
                else:
                    after(pe, o_ready, b, KV, c - 1)
                od = ps_vec[:, 0, :] if c % 2 else ps_od[:, :]
                for what in range(2):
                    for t in range(TT):
                        for g in range(GROUP):
                            rows = slice(HD * g, HD * (g + 1))
                            lhs = v_tok[:, t, HD * c:HD * (c + 1)] if what == 0 else ones[:, :]
                            rhs = prob0[:, c % 2, g, :] if t == 0 else prob1[:, c % 2, g, :]
                            mm = nc.tensor.matmul(od[rows, what * S + t * P:(what + 1) * S], lhs, rhs,
                                                  start=(t == 0), stop=(t == 1), tile_position=(0, HD * g))
                mm.then_inc(pv_done, 1)

            def out_product(b, t):
                if t == 0:
                    after(pe, otl_ready, b, KV, KV)
                tok = slice(t * P, (t + 1) * P)
                passes(ps_pair[:, t, :], [(ot_h[:, c, tok], ot_l[:, c, tok], wo_h[:, c * D:(c + 1) * D],
                                           wo_l[:, c * D:(c + 1) * D]) for c in range(DC)]).then_inc(wo_done, 1)

            def x_turn(f, t):
                after(pe, x_ready, f, TT, t + 1)
                if t == 0:
                    after(pe, utl_ready, f - 1, 2 * TT, 2 * TT)
                else:
                    after(pe, xl_ready, f, TT, 1)
                for c in range(DC):
                    mm = nc.tensor.transpose(ps_turn[:, c * P:(c + 1) * P], x[:, t, c * P:(c + 1) * P], ident[:, :])
                mm.then_inc(xt_done, 1)

            def vec_chunk(f, b, t, i):
                n, c = divmod(i, DC)
                if i == 0:
                    after(pe, xl_ready, f, TT, t + 1)
                    if t == 0 and b is not None:
                        after(pe, ql_ready, b, 2, 2)
                    elif t == 0:
                        after(pe, o_ready, f, KV, KV)
                    else:
                        after(pe, routed_ready, f, TT, t)
                w = slice(c * AR + n * 512, c * AR + (n + 1) * 512)
                for j, (lhs, rhs) in enumerate(((xt_h, at_h), (xt_h, at_l), (xt_l, at_h))):
                    mm = nc.tensor.matmul(ps_vec[:, n, :], lhs[:, t, c, :], rhs[:, w], start=(c == 0 and j == 0),
                                          stop=(c == DC - 1 and j == 2))
                if c == DC - 1:
                    mm.then_inc(vec_done, 1)

            def base_chunk(f, t, c):
                if c == 0:
                    after(pe, result_ready, f, TT, t)
                w = slice(c * D, (c + 1) * D)
                for j, (lhs, rhs) in enumerate(((xt_h, wt_h), (xt_h, wt_l), (xt_l, wt_h))):
                    nc.tensor.matmul(ps_acc[:, :], lhs[:, t, c, :], rhs[:, w], start=(c == 0 and j == 0), stop=False)

            def u_turn(f, t, h):
                if h == 0:
                    after(pe, u_ready, f, TT, t + 1)
                    if t == 0:
                        after(pe, xl_ready, f, TT, TT)
                after(pe, utl_ready, f, 2 * TT, 2 * t + h)
                for i in range(4):
                    k = 4 * h + i
                    mm = nc.tensor.transpose(ps_turn[:, i * P:(i + 1) * P], u[:, k * P:(k + 1) * P], ident[:, :])
                mm.then_inc(ut_done, 1)

            def delta_chunk(f, t, k):
                if k % 4 == 0:
                    after(pe, utl_ready, f, 2 * TT, 2 * t + k // 4 + 1)
                w = slice(k * D, (k + 1) * D)
                for j, (lhs, rhs) in enumerate(((ut_h, bt_h), (ut_h, bt_l), (ut_l, bt_h))):
                    mm = nc.tensor.matmul(ps_acc[:, :], lhs[:, k, :], rhs[:, w], start=False,
                                          stop=(k == RC - 1 and j == 2))
                if k == RC - 1:
                    mm.then_inc(acc_done, 1)

            def iteration(b, f, n):
                if f is not None:
                    for i in range(8):
                        vec_chunk(f, b, 0, i)
                        if i == 2:
                            x_turn(f, 1)
                    for c in range(DC):
                        base_chunk(f, 0, c)
                for i in range(8):
                    if f is not None:
                        vec_chunk(f, b, 1, i)
                        if i == 5:
                            u_turn(f, 0, 0)
                    if b is not None and i >= 1 and i < 7:
                        score(b, i - 1)
                if f is not None:
                    u_turn(f, 0, 1)
                if b is not None:
                    score(b, 6)
                    score(b, 7)
                if f is not None:
                    for k in range(RC):
                        delta_chunk(f, 0, k)
                if n is not None:
                    e_turn(n)
                for i in range(4):
                    if f is not None:
                        base_chunk(f, 1, i)
                    if b is not None:
                        score(b, 8 + i)
                if n is not None:
                    h0_product(n)
                if b is not None:
                    for i in range(12, HEADS):
                        score(b, i)
                    max_turn(b)
                if f is not None:
                    u_turn(f, 1, 0)
                    for k in range(0, 4):
                        delta_chunk(f, 1, k)
                    u_turn(f, 1, 1)
                if b is not None:
                    scores_t(b, 0)
                if f is not None:
                    for k in range(4, 6):
                        delta_chunk(f, 1, k)
                if b is not None:
                    scores_t(b, 1)
                    values(b, n, 0)
                if n is not None:
                    e2_turn(n)
                if b is not None:
                    scores_t(b, 2)
                    values(b, n, 1)
                    scores_t(b, 3)
                    values(b, n, 2)
                    values(b, n, 3)
                    for t in range(TT):
                        out_product(b, t)
                if n is not None:
                    qkv_product(n)
                if b is not None:
                    x_turn(b, 0)
                if f is not None:
                    for k in range(6, RC):
                        delta_chunk(f, 1, k)

            pe.wait_ge(const_pool, 11)
            pe.wait_ge(const_dve, 1)
            pe.wait_ge(set_dve, 4)
            for c in range(DC):
                mm = nc.tensor.transpose(ps_turn[:, c * P:c * P + EA], wc[0:EA, c * P:(c + 1) * P], ident[0:EA, 0:EA])
            mm.then_inc(set_pe, 1)
            pe.wait_ge(set_act, 2)
            pe.wait_ge(qkv_in, 48)
            for n, (lo, hi) in enumerate(((0, D), (D, QKV))):
                for c in range(DC):
                    mm = nc.tensor.matmul(ps_vec[0:EA, n, 0:hi - lo], wc_t[:, c, 0:EA], w_qkv[:, c, lo:hi],
                                          start=(c == 0), stop=(c == DC - 1))
            mm.then_inc(set_pe, 1)
            pe.wait_ge(set_dve, 6)
            e_turn(0)
            h0_product(0)
            e2_turn(0)
            qkv_product(0)
            pe.wait_ge(part_lo, len(pieces))
            iteration(0, None, 1)
            iteration(1, 0, 2)
            with pe.Fori(2, NB - 1) as b:
                iteration(b, b - 1, b + 1)
            iteration(NB - 1, NB - 2, None)
            iteration(None, NB - 1, None)


def kernel(x, L0_tok_emb, L0_tok_W, L0_tok_b, L0_attn_Wq, L0_attn_Wk, L0_attn_Wv, L0_attn_Wo,
           L0_ffn_A, L0_ffn_B, L0_ffn_W, L0_ffn_bias):
    import numpy as np
    import concourse.bacc as bacc
    from concourse.bass_utils import run_bass_kernel_spmd

    x = np.asarray(x)
    A = np.asarray(L0_ffn_A)
    B = np.asarray(L0_ffn_B)
    arrays = {
        "ids": np.ascontiguousarray(x.reshape(-1, 128).T),
        "emb": np.ascontiguousarray(L0_tok_emb),
        "w_tok": np.ascontiguousarray(L0_tok_W),
        "b_tok": np.ascontiguousarray(L0_tok_b),
        "w_q": np.ascontiguousarray(L0_attn_Wq),
        "w_k": np.ascontiguousarray(L0_attn_Wk),
        "w_v": np.ascontiguousarray(L0_attn_Wv),
        "w_o": np.ascontiguousarray(L0_attn_Wo),
        "a_t": np.ascontiguousarray(A.reshape(-1, A.shape[2]).T),
        "b_t": np.ascontiguousarray(B.transpose(0, 2, 1).reshape(-1, B.shape[1])),
        "w_t": np.ascontiguousarray(np.asarray(L0_ffn_W).T),
        "bias": np.ascontiguousarray(L0_ffn_bias),
    }
    nc = bacc.Bacc("TRN2", target_bir_lowering=False, num_devices=1)
    args = [nc.dram_tensor(n, a.shape, mybir.dt.from_np(a.dtype), kind="ExternalInput").ap() for n, a in arrays.items()]
    out = nc.dram_tensor("out", (x.size, L0_tok_W.shape[1]), F32, kind="ExternalOutput").ap()
    tower_kernel(nc, *args, out)
    r = run_bass_kernel_spmd(nc, [arrays], core_ids=[0])
    return r.results[0]["out"].reshape(*x.shape, -1)
```

```python
from contextlib import ExitStack

import concourse.bass as bass
from concourse import mybir

F32 = mybir.dt.float32
F32R = mybir.dt.float32r
BF16 = mybir.dt.bfloat16
I32 = mybir.dt.int32
U32 = mybir.dt.uint32
ALU = mybir.AluOpType
ACT = mybir.ActivationFunctionType
AX = mybir.AxisListType

P = 128
HEADS = 16
KV = 4
GROUP = HEADS // KV
TOPK = 4
EPS = 1e-5
NEVER = -1e30
LARGEST = 3e38


def tower_kernel(nc, ids, emb, w_tok, b_tok, w_q, w_k, w_v, w_o, a_t, b_t, w_t, bias, out):
    EMB = emb.shape[1]
    EA = EMB + 1
    D = w_tok.shape[1]
    DC = D // P
    NT = ids.shape[1]
    TT = 2
    S = TT * P
    NB = NT // TT
    HD = D // HEADS
    KD = KV * HD
    QKV = D + 2 * KD
    AR = a_t.shape[1]
    NA = AR // 16
    R = AR // NA
    RC = AR // P
    ROOT = float(D) ** 0.5
    QSCALE = float(HD) ** -0.5
    assert HD == 32 and KD == P and S == 256 and D == 512 and AR == 1024 and RC == 8
    QSTACK = 3 * HD
    STACK = QSTACK + 2

    with ExitStack() as ctx:
        def sb(name, shape, dt=F32):
            return ctx.enter_context(nc.sbuf_tensor(name, shape, dt))

        def psum(name, shape, dt=F32):
            return ctx.enter_context(nc.psum_tensor(name, shape, dt))

        def sem(name):
            return ctx.enter_context(nc.semaphore(name))

        ps_pair = psum("ps_pair", [P, 2, 512])
        ps_small = psum("ps_small", [P, 512])
        ps_vec = psum("ps_vec", [P, 3, 512])
        ps_acc = psum("ps_acc", [P, 512])
        ps_turn = psum("ps_turn", [P, 512])

        ident = sb("ident", [P, P])
        mask = sb("mask", [P, S])
        ident_b = sb("ident_b", [P, P], BF16)
        mask_t = sb("mask_t", [P, P], BF16)
        ones = mask[:, 0:HD]
        minus_half = sb("minus_half", [P, TT])
        bias_rows = sb("bias_rows", [P, D])
        idx_all = sb("idx_all", [P, NT + TT], I32)
        idx_now = sb("idx_now", [P, TT], I32)

        shared_a = sb("shared_a", [P, 8 * D])
        stage = shared_a[:, :].rearrange("p (i n) -> p i n", i=2)
        result = shared_a[:, 0:2 * D].rearrange("p (t n) -> p t n", t=TT)
        x = shared_a[:, 2 * D:4 * D].rearrange("p (t n) -> p t n", t=TT)
        squares = shared_a[:, 4 * D:4 * D + AR]
        routed = squares
        u = shared_a[:, 6 * D:6 * D + AR]
        shared_b = sb("shared_b", [P, 2 * TT * D])
        w_query = shared_b[:, :].rearrange("p (c n) -> p c n", c=DC)
        h0 = shared_b[:, 0:TT * D].rearrange("p (t n) -> p t n", t=TT)
        h1 = shared_b[:, TT * D:2 * TT * D].rearrange("p (t n) -> p t n", t=TT)
        prob0 = sb("prob0", [P, 2, GROUP, S])
        prob1 = sb("prob1", [P, 2, GROUP, P])
        wc = prob0[:, 0, :, :].rearrange("p g s -> p (g s)")[:, 0:D]
        w_emb = prob0[:, 0, :, :].rearrange("p g s -> p (g s)")[:, D:2 * D]
        wc_t = prob0[:, 1, :, :].rearrange("p g s -> p (g s)")[:, 0:D]
        wc_t = wc_t.rearrange("p (c n) -> p c n", c=DC)
        w_kv = prob1[:, :, :, :].rearrange("p i g s -> p (i g s)").rearrange("p (c n) -> p c n", c=DC)
        w_mean = sb("w_mean", [P, 2])
        we_h = sb("we_h", [P, D], F32R)
        we_l = sb("we_l", [P, D], F32R)
        m_h = sb("m_h", [P, QKV], F32R)
        m_l = sb("m_l", [P, QKV], F32R)
        wo_h = sb("wo_h", [P, DC * D], F32R)
        wo_l = sb("wo_l", [P, DC * D], F32R)
        at_h = sb("at_h", [P, DC * AR], F32R)
        at_l = sb("at_l", [P, DC * AR], F32R)
        wt_h = sb("wt_h", [P, DC * D], F32R)
        wt_l = sb("wt_l", [P, DC * D], F32R)
        bt_h = sb("bt_h", [P, RC * D], F32R)
        bt_l = sb("bt_l", [P, RC * D], F32R)

        h0_next = sb("h0_next", [P, TT, D])
        e_tok = sb("e_tok", [P, TT, EA])
        e_scaled = sb("e_scaled", [P, TT, EA])
        et_h = sb("et_h", [P, S], F32R)
        et_l = sb("et_l", [P, S], F32R)
        e2_h = sb("e2_h", [P, S], F32R)
        e2_l = sb("e2_l", [P, S], F32R)
        stats = sb("stats", [P, TT, 6])
        mean_var = sb("mean_var", [P, TT, 2])
        var_eps = sb("var_eps", [P, TT])
        rstd = sb("rstd", [P, TT])
        q_h = sb("q_h", [P, TT, KV, P], F32R)
        q_l = sb("q_l", [P, TT, KV, P], F32R)
        k_h = sb("k_h", [P, S], F32R)
        k_l = sb("k_l", [P, S], F32R)
        q_stack = sb("q_stack", [P, TT, GROUP, KV, P], F32R)
        k_stack = sb("k_stack", [P, KV, S], F32R)
        v_tok = sb("v_tok", [P, TT, KD])
        row_max = sb("row_max", [P, TT, HEADS])
        m_rows_h = sb("m_rows_h", [TT * HEADS, P], F32R)
        m_rows_l = sb("m_rows_l", [TT * HEADS, P], F32R)
        rden = sb("rden", [P, S])
        o_t = sb("o_t", [P, 2, S])
        ot_h, ot_l = (q[:, :, :, :].rearrange("p t c q -> p (t c q)").rearrange("p (c s) -> p c s", c=KV)
                      for q in (q_h, q_l))

        stats2 = sb("stats2", [P, TT, 6])
        mean_var2 = sb("mean_var2", [P, TT, 2])
        var_eps2 = sb("var_eps2", [P, TT])
        rstd2 = sb("rstd2", [P, TT])
        xt_h = sb("xt_h", [P, TT, DC, P], F32R)
        xt_l = sb("xt_l", [P, TT, DC, P], F32R)
        ut_h = sb("ut_h", [P, RC, P], F32R)
        arrows = sb("arrows", [P, NA + TOPK])
        top8 = sb("top8", [P, 8])
        struck = sb("struck", [P, NA + TOPK])
        route = sb("route", [P, NA])
        v_sum = sb("v_sum", [P, R])
        ut_l = sb("ut_l", [P, RC, P], F32R)

        passed = sem("passed")
        const_pool = sem("const_pool")
        const_dve = sem("const_dve")
        idx_in = sem("idx_in")
        small_in = sem("small_in")
        qkv_in = sem("qkv_in")
        bias_in = sem("bias_in")
        big_in = [sem("big_in0"), sem("big_in1")]
        set_dve = sem("set_dve")
        set_act = sem("set_act")
        set_pe = sem("set_pe")
        part_hi = sem("part_hi")
        part_lo = sem("part_lo")

        idx_ready = sem("idx_ready")
        gathered = sem("gathered")
        et_done = sem("et_done")
        eth_ready = sem("eth_ready")
        etl_ready = sem("etl_ready")
        h0_done = sem("h0_done")
        h0_ready = sem("h0_ready")
        h0_moved = sem("h0_moved")
        dve_attn = sem("dve_attn")
        mv_ready = sem("mv_ready")
        eps_ready = sem("eps_ready")
        rstd_ready = sem("rstd_ready")
        e2_ready = sem("e2_ready")
        e2t_done = sem("e2t_done")
        e2h_ready = sem("e2h_ready")
        e2l_ready = sem("e2l_ready")
        k_done = sem("k_done")
        q_done = sem("q_done")
        v_done = sem("v_done")
        kh_ready = sem("kh_ready")
        kl_ready = sem("kl_ready")
        qh_ready = sem("qh_ready")
        ql_ready = sem("ql_ready")
        v_ready = sem("v_ready")
        stacked = [sem(f"stacked{j}") for j in range(KV)]
        s_done = sem("s_done")
        max_ready = sem("max_ready")
        mt_done = sem("mt_done")
        mh_ready = sem("mh_ready")
        ml_ready = sem("ml_ready")
        m_stacked = sem("m_stacked")
        st_done = sem("st_done")
        exp_ready = sem("exp_ready")
        pv_done = sem("pv_done")
        rden_ready = sem("rden_ready")
        o_ready = sem("o_ready")
        oth_ready = sem("oth_ready")
        otl_ready = sem("otl_ready")
        wo_done = sem("wo_done")
        h1_ready = sem("h1_ready")
        stats2_ready = sem("stats2_ready")
        mv2_ready = sem("mv2_ready")
        eps2_ready = sem("eps2_ready")
        rstd2_ready = sem("rstd2_ready")
        x_ready = sem("x_ready")
        hb_ready = sem("hb_ready")

        xt_done = sem("xt_done")
        xh_ready = sem("xh_ready")
        xl_ready = sem("xl_ready")
        vec_done = sem("vec_done")
        sq_ready = sem("sq_ready")
        dve_route = sem("dve_route")
        route_ready = sem("route_ready")
        routed_ready = sem("routed_ready")
        vsum_ready = sem("vsum_ready")
        u_ready = sem("u_ready")
        ut_done = sem("ut_done")
        uth_ready = sem("uth_ready")
        utl_ready = sem("utl_ready")
        acc_done = sem("acc_done")
        result_ready = sem("result_ready")
        stored = [sem("stored0"), sem("stored1")]

        def after(eng, s, b, per, k):
            n = b * per + k
            if isinstance(n, int) and n <= 0:
                return
            eng.wait_ge(s, n)

        def after_apart(eng, s, b, per, k):
            after(eng, s, b, per, k)
            if not isinstance(b, int):
                eng.sem_inc(passed, 1)

        n_stack = 6 * 16
        n_mrow = 2 * 16
        heads = [(g, c) for j in range(KV) for g in range(j + 1) for c in range(j + 1) if j in (g, c)]

        pieces = []
        for weight, hi, lo, n in ((w_o, wo_h, wo_l, 1), (a_t, at_h, at_l, 2), (w_t, wt_h, wt_l, 1), (b_t, bt_h, bt_l, 2)):
            src = weight.rearrange("(c p) n -> p c n", p=P)
            c = src.shape[1] // n
            for i in range(n):
                w = 4 * D
                pieces.append((src[:, i * c:(i + 1) * c, :], hi[:, i * w:(i + 1) * w], lo[:, i * w:(i + 1) * w]))

        block = ctx.enter_context(nc.Block())

        @block.sync
        def _(sp):
            sp.dma_start(idx_all[:, 0:NT], ids).then_inc(idx_in, 16)
            sp.dma_start(w_emb[0:EMB, :], w_tok).then_inc(small_in, 16)
            sp.dma_start(w_emb[EMB:EA, :], b_tok.rearrange("(o n) -> o n", o=1)).then_inc(small_in, 16)
            sp.dma_start(w_query, w_q.rearrange("(c p) n -> p c n", p=P)).then_inc(qkv_in, 16)
            sp.dma_start(w_kv[:, :, 0:KD], w_k.rearrange("(c p) n -> p c n", p=P)).then_inc(qkv_in, 16)
            sp.dma_start(w_kv[:, :, KD:2 * KD], w_v.rearrange("(c p) n -> p c n", p=P)).then_inc(qkv_in, 16)
            sp.dma_start(bias_rows[:, :], bias.rearrange("(o n) -> o n", o=1).broadcast_to([P, D])).then_inc(bias_in, 16)

            def load_piece(i):
                if i >= 2:
                    sp.wait_ge(part_lo, i - 1)
                src = pieces[i][0]
                dst = stage[:, i % 2, :].rearrange("p (c n) -> p c n", n=src.shape[2])
                sp.dma_start(dst, src).then_inc(big_in[i % 2], 16)

            load_piece(0)
            load_piece(1)

            def stack(b, j):
                if j == 0:
                    after_apart(sp, st_done, b - 1, 3 * KV, 3 * KV)
                    after_apart(sp, kl_ready, b, 1, 1)
                    after_apart(sp, ql_ready, b, 2, 2)
                rows = slice(HD * j, HD * (j + 1))
                for slot, part in enumerate((k_h, k_l, k_h)):
                    sp.dma_start(k_stack[HD * slot:HD * (slot + 1), j, :].bitcast(F32),
                                 part[rows, :].bitcast(F32)).then_inc(stacked[j], 16)
                for slot, part in enumerate((q_h, q_h, q_l)):
                    sp.dma_start(q_stack[HD * slot:HD * (slot + 1), :, j, :, :].bitcast(F32),
                                 part[rows, :, :, :].bitcast(F32)).then_inc(stacked[j], 16)

            def stack_max(b):
                for slot, (part, ready) in enumerate(((m_rows_h, mh_ready), (m_rows_l, ml_ready))):
                    after_apart(sp, ready, b, 1, 1)
                    row = q_stack[QSTACK + slot:QSTACK + slot + 1, :, :, :, :]
                    sp.dma_start(row.rearrange("o t g c q -> o (t g c) q").bitcast(F32),
                                 part[:, :].bitcast(F32)).then_inc(m_stacked, 16)

            def store(f, t):
                after_apart(sp, result_ready, f, TT, t + 1)
                sp.dma_start(out[bass.ds(f * S + t * P, P), :], result[:, t, :]).then_inc(stored[t], 16)

            def iteration(b, f, n):
                if f is not None:
                    store(f, 0)
                if b is not None:
                    stack_max(b)
                if f is None:
                    load_piece(4)
                    load_piece(5)
                if n is not None:
                    stack(n, 0)
                if f is not None:
                    store(f, 1)
                if n is not None:
                    for j in range(1, KV):
                        stack(n, j)

            for j in range(KV):
                stack(0, j)
            load_piece(2)
            load_piece(3)
            iteration(0, None, 1)
            iteration(1, 0, 2)
            with sp.Fori(2, NB - 1) as b:
                iteration(b, b - 1, b + 1)
            iteration(NB - 1, NB - 2, None)
            iteration(None, NB - 1, None)
            for t in range(TT):
                sp.wait_ge(stored[t], 16 * NB)

        @block.gpsimd
        def _(pool):
            nc.gpsimd.memset(ident[:, :], 0.0).then_inc(const_pool, 1)
            nc.gpsimd.memset(mask[:, :], 1.0).then_inc(const_pool, 1)
            nc.gpsimd.memset(minus_half[:, :], -0.5).then_inc(const_pool, 1)
            nc.gpsimd.memset(idx_all[:, NT:NT + TT], 0).then_inc(const_pool, 1)
            nc.gpsimd.memset(e_tok[:, :, EMB:EA], 1.0).then_inc(const_pool, 1)
            nc.gpsimd.memset(ident_b[:, :], 0.0).then_inc(const_pool, 1)
            nc.gpsimd.memset(mask_t[:, :], 0.0).then_inc(const_pool, 1)
            pool.wait_ge(const_pool, 7)
            nc.gpsimd.affine_select(out=ident_b[:, :], in_=ident_b[:, :], compare_op=ALU.not_equal, fill=1.0,
                                    base=0, pattern=[[-1, P]], channel_multiplier=1).then_inc(const_pool, 1)
            nc.gpsimd.affine_select(out=mask_t[:, :], in_=mask_t[:, :], compare_op=ALU.is_ge, fill=NEVER,
                                    base=0, pattern=[[1, P]], channel_multiplier=-1).then_inc(const_pool, 1)
            nc.gpsimd.affine_select(out=ident[:, :], in_=ident[:, :], compare_op=ALU.not_equal, fill=1.0,
                                    base=0, pattern=[[-1, P]], channel_multiplier=1).then_inc(const_pool, 1)
            nc.gpsimd.affine_select(out=mask[:, P:S], in_=mask[:, P:S], compare_op=ALU.is_ge, fill=NEVER,
                                    base=0, pattern=[[-1, P]], channel_multiplier=1).then_inc(const_pool, 1)

            def gather(b):
                after(pool, e2_ready, b - 1, TT, TT)
                after(pool, gathered, b - 1, 16 * TT, 16 * TT)
                nc.gpsimd.tensor_copy(idx_now[:, :], idx_all[:, bass.ds(b * TT, TT)]).then_inc(idx_ready, 1)
                after_apart(pool, idx_ready, b, 1, 1)
                for t in range(TT):
                    nc.gpsimd.indirect_dma_start(
                        out=e_tok[:, t, 0:EMB], out_offset=None, in_=emb,
                        in_offset=bass.IndirectOffsetOnAxis(ap=idx_now[:, t:t + 1].bitcast(U32), axis=0),
                    ).then_inc(gathered, 16)

            def rstd_attn(b):
                after_apart(pool, mv_ready, b, TT, TT)
                nc.gpsimd.tensor_scalar_add(var_eps[:, :], mean_var[:, :, 1], EPS).then_inc(eps_ready, 1)
                after(pool, eps_ready, b, 1, 1)
                nc.gpsimd.tensor_tensor(rstd[:, :], var_eps[:, :], minus_half[:, :], ALU.pow).then_inc(rstd_ready, 1)

            def rstd_ffn(b, t):
                after_apart(pool, mv2_ready, b, TT, t + 1)
                nc.gpsimd.tensor_scalar_add(var_eps2[:, t:t + 1], mean_var2[:, t, 1:2], EPS).then_inc(eps2_ready, 1)
                after(pool, eps2_ready, b, TT, t + 1)
                nc.gpsimd.tensor_tensor(rstd2[:, t:t + 1], var_eps2[:, t:t + 1], minus_half[:, 0:1],
                                        ALU.pow).then_inc(rstd2_ready, 1)

            def add_bias(b, t):
                after(pool, stored[t], b, 16, 0)
                nc.gpsimd.tensor_tensor(result[:, t, :], h1[:, t, :], bias_rows[:, :], ALU.add).then_inc(hb_ready, 1)

            def spread(f, t):
                after(pool, vsum_ready, f, TT, t + 1)
                after(pool, ut_done, f, 2 * TT, 2 * t)
                nc.gpsimd.tensor_tensor(u[:, :].rearrange("p (a r) -> p a r", r=R),
                                        route[:, :].unsqueeze(2).broadcast_to([P, NA, R]),
                                        v_sum[:, :].unsqueeze(1).broadcast_to([P, NA, R]),
                                        ALU.mult).then_inc(u_ready, 1)

            def iteration(b, f, n):
                if f is not None:
                    spread(f, 0)
                    spread(f, 1)
                if n is not None:
                    rstd_attn(n)
                    gather(n + 1)
                if b is not None:
                    for t in range(TT):
                        rstd_ffn(b, t)
                    for t in range(TT):
                        add_bias(b, t)

            pool.wait_ge(idx_in, 16)
            gather(0)
            rstd_attn(0)
            gather(1)
            pool.wait_ge(bias_in, 16)
            iteration(0, None, 1)
            iteration(1, 0, 2)
            with pool.Fori(2, NB - 1) as b:
                iteration(b, b - 1, b + 1)
            iteration(NB - 1, NB - 2, None)
            iteration(None, NB - 1, None)
            pool.wait_ge(gathered, (NB + 1) * 16 * TT)

        @block.scalar
        def _(act):
            def e_hi(b):
                after(act, et_done, b, 1, 1)
                nc.scalar.copy(et_h[0:EA, :], ps_small[0:EA, 0:S]).then_inc(eth_ready, 1)

            def h0_out(b):
                after(act, h0_moved, b, TT, 0)
                for t in range(TT):
                    after(act, h0_done, b, TT, t + 1)
                    nc.scalar.mul(h0_next[:, t, :], ps_vec[:, 0, :], ROOT).then_inc(h0_ready, 1)

            def h0_move(b):
                after(act, h0_ready, b, TT, TT)
                for t in range(TT):
                    after(act, h1_ready, b - 1, TT, t + 1)
                    nc.scalar.copy(h0[:, t, :], h0_next[:, t, :]).then_inc(h0_moved, 1)

            def e2_hi(b):
                after(act, e2t_done, b, 1, 1)
                nc.scalar.copy(e2_h[0:EA, :], ps_turn[0:EA, 0:S]).then_inc(e2h_ready, 1)

            def qkv_hi(b):
                for j in range(KV):
                    after(act, stacked[j], b - 1, n_stack, n_stack)
                after(act, k_done, b, 1, 1)
                nc.scalar.copy(k_h[:, :], ps_small[:, 0:S]).then_inc(kh_ready, 1)
                after(act, wo_done, b - 1, TT, TT)
                for i in range(2):
                    after(act, q_done, b, 2, i + 1)
                    nc.scalar.copy(q_h[:, :, 2 * i:2 * i + 2, :].rearrange("p t c q -> p c t q"),
                                   ps_vec[:, i, :].rearrange("p (c t q) -> p c t q", c=2, t=TT)).then_inc(qh_ready, 1)
                after(act, pv_done, b - 1, KV, KV)
                after(act, v_done, b, 1, 1)
                nc.scalar.copy(v_tok[:, :, :],
                               ps_vec[:, 2, :].rearrange("p (t n) -> p t n", t=TT)[:, :, KD:2 * KD]).then_inc(v_ready, 1)

            def m_hi(b):
                after(act, mt_done, b, 1, 1)
                nc.scalar.mul(m_rows_h[:, :], ps_vec[0:TT * HEADS, 0, 0:P], -1.0).then_inc(mh_ready, 1)

            def exps(b, c):
                after(act, pv_done, b, KV, c - 1)
                for i in range(2):
                    after(act, st_done, b, 3 * KV, 3 * c + i + 1)
                    nc.scalar.activation(prob0[:, c % 2, 2 * i:2 * i + 2, :].rearrange("p g q -> p (g q)"),
                                         ps_pair[:, i, :], ACT.Exp, bias=ones[:, 0:1]).then_inc(exp_ready, 1)
                after(act, st_done, b, 3 * KV, 3 * c + 3)
                nc.scalar.activation(prob1[:, c % 2, :, :].rearrange("p g q -> p (g q)"), ps_small[:, :], ACT.Exp,
                                     bias=ones[:, 0:1]).then_inc(exp_ready, 1)

            def o_hi(b, c):
                after(act, o_ready, b, KV, c + 1)
                nc.scalar.copy(ot_h[:, c, :], o_t[:, c % 2, :]).then_inc(oth_ready, 1)

            def x_hi(f, t):
                after(act, acc_done, f - 1, TT, t + 1)
                after(act, xt_done, f, TT, t + 1)
                nc.scalar.copy(xt_h[:, t, :, :].rearrange("p c s -> p (c s)"), ps_turn[:, :]).then_inc(xh_ready, 1)

            def square(f, t, n):
                first = n == t
                if first:
                    after(act, vsum_ready, f, TT, t)
                after(act, vec_done, f, 2 * TT, 2 * t + (1 if first else 2))
                nc.scalar.activation(squares[:, n * 512:(n + 1) * 512], ps_vec[:, t + n, :], ACT.Square).then_inc(sq_ready, 1)

            def ut_hi(f, t, h):
                if h == 0:
                    after(act, acc_done, f, TT, t)
                after(act, ut_done, f, 2 * TT, 2 * t + h + 1)
                nc.scalar.copy(ut_h[:, 4 * h:4 * h + 4, :].rearrange("p c s -> p (c s)"),
                               (ps_turn, ps_small)[h][:, :]).then_inc(uth_ready, 1)

            def split(i):
                act.wait_ge(big_in[i % 2], 16 * (i // 2 + 1))
                nc.scalar.copy(pieces[i][1], stage[:, i % 2, :]).then_inc(part_hi, 1)

            def iteration(b, f, n):
                if n is not None:
                    e_hi(n)
                if f is not None:
                    x_hi(f, 1)
                    square(f, 0, 0)
                    square(f, 0, 1)
                    square(f, 1, 1)
                    square(f, 1, 0)
                    ut_hi(f, 0, 0)
                    ut_hi(f, 0, 1)
                if n is not None:
                    h0_out(n)
                if f is not None:
                    ut_hi(f, 1, 0)
                if b is not None:
                    m_hi(b)
                if f is not None:
                    ut_hi(f, 1, 1)
                if f is None:
                    split(2)
                    split(3)
                if b is not None:
                    exps(b, 0)
                    exps(b, 1)
                    exps(b, 2)
                    o_hi(b, 0)
                if n is not None:
                    e2_hi(n)
                if b is not None:
                    exps(b, 3)
                    o_hi(b, 1)
                if f is None:
                    split(4)
                if b is not None:
                    o_hi(b, 2)
                    o_hi(b, 3)
                if n is not None:
                    qkv_hi(n)
                if b is not None:
                    x_hi(b, 0)
                if n is not None:
                    h0_move(n)
                if f is None:
                    split(5)

            act.wait_ge(small_in, 32)
            act.wait_ge(const_dve, 1)
            nc.scalar.copy(we_h[0:EA, :], w_emb[0:EA, :]).then_inc(set_act, 1)
            act.wait_ge(set_pe, 1)
            nc.scalar.copy(wc_t[:, :, 0:EA], ps_turn[:, :].rearrange("p (c n) -> p c n", c=DC)[:, :, 0:EA]).then_inc(set_act, 1)
            e_hi(0)
            h0_out(0)
            act.wait_ge(set_pe, 2)
            nc.scalar.mul(m_h[0:EA, 0:D], ps_vec[0:EA, 1, :], QSCALE).then_inc(set_act, 1)
            nc.scalar.copy(m_h[0:EA, D:QKV], ps_vec[0:EA, 2, 0:QKV - D]).then_inc(set_act, 1)
            e2_hi(0)
            h0_move(0)
            qkv_hi(0)
            split(0)
            split(1)
            iteration(0, None, 1)
            act.wait_ge(part_lo, len(pieces))
            iteration(1, 0, 2)
            with act.Fori(2, NB - 1) as b:
                iteration(b, b - 1, b + 1)
            iteration(NB - 1, NB - 2, None)
            iteration(None, NB - 1, None)

        @block.vector
        def _(dve):
            def e_lo(b):
                after(dve, eth_ready, b, 1, 1)
                nc.vector.tensor_tensor(et_l[0:EA, :], ps_small[0:EA, 0:S], et_h[0:EA, :].bitcast(F32),
                                        ALU.subtract).then_inc(etl_ready, 1)

            def norm_stats(b):
                for t in range(TT):
                    after(dve, h0_ready, b, TT, t + 1)
                    nc.vector.bn_stats(stats[:, t, :], h0_next[:, t, :]).then_inc(dve_attn, 1)
                for t in range(TT):
                    after_apart(dve, dve_attn, b, TT, t + 1)
                    nc.vector.bn_aggr(mean_var[:, t, :], stats[:, t, :]).then_inc(mv_ready, 1)

            def e_scale(b):
                after(dve, rstd_ready, b, 1, 1)
                for t in range(TT):
                    nc.vector.tensor_scalar(e_scaled[:, t, :], e_tok[:, t, :], rstd[:, t:t + 1], ROOT,
                                            ALU.mult, ALU.mult).then_inc(e2_ready, 1)

            def e2_lo(b):
                after(dve, e2h_ready, b, 1, 1)
                nc.vector.tensor_tensor(e2_l[0:EA, :], ps_turn[0:EA, 0:S], e2_h[0:EA, :].bitcast(F32),
                                        ALU.subtract).then_inc(e2l_ready, 1)

            def k_lo(b):
                after(dve, kh_ready, b, 1, 1)
                nc.vector.tensor_tensor(k_l[:, :], ps_small[:, 0:S], k_h[:, :].bitcast(F32),
                                        ALU.subtract).then_inc(kl_ready, 1)

            def q_lo(b, i):
                after(dve, qh_ready, b, 2, i + 1)
                part = slice(2 * i, 2 * i + 2)
                nc.vector.tensor_tensor(q_l[:, :, part, :].rearrange("p t c q -> p c t q"),
                                        ps_vec[:, i, :].rearrange("p (c t q) -> p c t q", c=2, t=TT),
                                        q_h[:, :, part, :].rearrange("p t c q -> p c t q").bitcast(F32),
                                        ALU.subtract).then_inc(ql_ready, 1)

            def maximum(b, n):
                g, c = heads[n]
                col = KV * g + c
                after_apart(dve, s_done, b, HEADS, n + 1)
                nc.vector.tensor_tensor_reduce(out=ps_pair[:, n % 2, 0:P], in0=ps_pair[:, n % 2, 0:P], in1=mask[:, P:S],
                                               scale=1.0, scalar=-LARGEST, op0=ALU.add, op1=ALU.max,
                                               accum_out=row_max[:, 0, col:col + 1])
                nc.vector.tensor_tensor_reduce(out=ps_pair[:, n % 2, S:2 * S], in0=ps_pair[:, n % 2, S:2 * S], in1=mask[:, :],
                                               scale=1.0, scalar=-LARGEST, op0=ALU.add, op1=ALU.max,
                                               accum_out=row_max[:, 1, col:col + 1]).then_inc(max_ready, 1)

            def m_lo(b):
                after(dve, mh_ready, b, 1, 1)
                nc.vector.scalar_tensor_tensor(out=m_rows_l[:, :], in0=ps_vec[0:TT * HEADS, 0, 0:P], scalar=-1.0,
                                               in1=m_rows_h[:, :].bitcast(F32), op0=ALU.mult,
                                               op1=ALU.subtract).then_inc(ml_ready, 1)

            def normalise(b, c):
                od = ps_vec[:, 2 - c % 2, :]
                after(dve, pv_done, b, KV, c + 1)
                after(dve, o_ready, b, KV, c)
                nc.vector.reciprocal(rden[:, :], od[:, S:2 * S]).then_inc(rden_ready, 1)
                if c > 0:
                    o_lo(b, c - 1)
                after(dve, otl_ready, b, KV, c - 1)
                after(dve, rden_ready, b, KV, c + 1)
                nc.vector.tensor_tensor(o_t[:, c % 2, :], od[:, 0:S], rden[:, :], ALU.mult).then_inc(o_ready, 1)

            def o_lo(b, c):
                after(dve, oth_ready, b, KV, c + 1)
                nc.vector.tensor_tensor(ot_l[:, c, :], o_t[:, c % 2, :], ot_h[:, c, :].bitcast(F32),
                                        ALU.subtract).then_inc(otl_ready, 1)

            def residual(b, t):
                after(dve, hb_ready, b - 1, TT, t + 1)
                after(dve, h0_moved, b, TT, t + 1)
                after(dve, wo_done, b, TT, t + 1)
                nc.vector.tensor_tensor(h1[:, t, :], ps_pair[:, t, :], h0[:, t, :], ALU.add).then_inc(h1_ready, 1)
                after(dve, h1_ready, b, TT, t + 1)
                nc.vector.bn_stats(stats2[:, t, :], h1[:, t, :]).then_inc(stats2_ready, 1)
                after_apart(dve, stats2_ready, b, TT, t + 1)
                nc.vector.bn_aggr(mean_var2[:, t, :], stats2[:, t, :]).then_inc(mv2_ready, 1)

            def norm_x(b, t):
                after(dve, rstd2_ready, b, TT, t + 1)
                nc.vector.tensor_scalar(x[:, t, :], h1[:, t, :], mean_var2[:, t, 0:1], rstd2[:, t:t + 1],
                                        ALU.subtract, ALU.mult).then_inc(x_ready, 1)

            def x_lo(f, t):
                after(dve, xh_ready, f, TT, t + 1)
                nc.vector.tensor_tensor(xt_l[:, t, :, :].rearrange("p c s -> p (c s)"), ps_turn[:, :],
                                        xt_h[:, t, :, :].rearrange("p c s -> p (c s)").bitcast(F32),
                                        ALU.subtract).then_inc(xl_ready, 1)

            def norms(f, t):
                for i, n in enumerate((t, 1 - t)):
                    half = slice(n * NA // 2, (n + 1) * NA // 2)
                    after(dve, sq_ready, f, 2 * TT, 2 * t + i + 1)
                    nc.vector.tensor_reduce(out=arrows[:, half],
                                            in_=squares[:, n * 512:(n + 1) * 512].rearrange("p (a r) -> p a r", r=R),
                                            axis=AX.X, op=ALU.add).then_inc(dve_route, 1)

            def choose(f, t):
                after_apart(dve, dve_route, f, 4 * TT, 4 * t + 2)
                nc.vector.max(out=top8[:, :], in_=arrows[:, :]).then_inc(dve_route, 1)

            def strike(f, t):
                after_apart(dve, dve_route, f, 4 * TT, 4 * t + 3)
                nc.vector.match_replace(out=struck[:, :], in_to_replace=top8[:, :], in_values=arrows[:, :],
                                        imm_value=-1.0).then_inc(dve_route, 1)

            def select(f, t):
                after(dve, u_ready, f, TT, t)
                after(dve, dve_route, f, 4 * TT, 4 * t + 4)
                nc.vector.tensor_scalar(route[:, :], struck[:, 0:NA], -1.0, 1.0 / TOPK, ALU.is_equal,
                                        ALU.mult).then_inc(route_ready, 1)

            def route_arrows(f, t):
                after(dve, route_ready, f, TT, t + 1)
                nc.vector.tensor_tensor(routed[:, :].rearrange("p (a r) -> p a r", r=R),
                                        ps_vec[:, t:t + 2, :].rearrange("p i (a r) -> p (i a) r", r=R),
                                        route[:, :].unsqueeze(2).broadcast_to([P, NA, R]),
                                        ALU.mult).then_inc(routed_ready, 1)

            def sum_arrows(f, t):
                after(dve, routed_ready, f, TT, t + 1)
                nc.vector.tensor_reduce(out=v_sum[:, :], in_=routed[:, :].rearrange("p (a r) -> p r a", r=R),
                                        axis=AX.X, op=ALU.add).then_inc(vsum_ready, 1)

            def ut_lo(f, t, h):
                after(dve, uth_ready, f, 2 * TT, 2 * t + h + 1)
                nc.vector.tensor_tensor(ut_l[:, 4 * h:4 * h + 4, :].rearrange("p c s -> p (c s)"),
                                        (ps_turn, ps_small)[h][:, :],
                                        ut_h[:, 4 * h:4 * h + 4, :].rearrange("p c s -> p (c s)").bitcast(F32),
                                        ALU.subtract).then_inc(utl_ready, 1)

            def finish(f, t):
                after(dve, hb_ready, f, TT, t + 1)
                after(dve, acc_done, f, TT, t + 1)
                nc.vector.tensor_tensor(result[:, t, :], ps_acc[:, :], result[:, t, :], ALU.add).then_inc(result_ready, 1)

            def split(i):
                _, hi, lo = pieces[i]
                dve.wait_ge(part_hi, i + 1)
                nc.vector.tensor_tensor(lo, stage[:, i % 2, :], hi.bitcast(F32), ALU.subtract).then_inc(part_lo, 1)

            def iteration(b, f, n):
                if n is not None:
                    e_lo(n)
                if f is not None:
                    x_lo(f, 1)
                    norms(f, 0)
                    choose(f, 0)
                    strike(f, 0)
                    select(f, 0)
                    route_arrows(f, 0)
                    sum_arrows(f, 0)
                if b is not None:
                    for i in range(7):
                        maximum(b, i)
                if f is not None:
                    ut_lo(f, 0, 0)
                if b is not None:
                    maximum(b, 7)
                if f is not None:
                    ut_lo(f, 0, 1)
                for i, step in ((8, norms), (9, choose), (10, strike)):
                    if f is not None:
                        step(f, 1)
                    if b is not None:
                        maximum(b, i)
                if f is not None:
                    select(f, 1)
                    route_arrows(f, 1)
                if b is not None:
                    maximum(b, 11)
                if b is None:
                    sum_arrows(f, 1)
                    finish(f, 0)
                elif f is not None:
                    finish(f, 0)
                    sum_arrows(f, 1)
                if b is not None:
                    for i in range(12, HEADS):
                        maximum(b, i)
                if f is not None:
                    ut_lo(f, 1, 0)
                if b is not None:
                    m_lo(b)
                if f is not None:
                    ut_lo(f, 1, 1)
                else:
                    split(2)
                    split(3)
                if n is not None:
                    norm_stats(n)
                    e_scale(n)
                if b is not None:
                    normalise(b, 0)
                    normalise(b, 1)
                if n is not None:
                    e2_lo(n)
                if b is not None:
                    normalise(b, 2)
                    normalise(b, 3)
                    o_lo(b, KV - 1)
                if f is None:
                    split(4)
                if b is not None:
                    residual(b, 0)
                if n is not None:
                    k_lo(n)
                if b is not None:
                    norm_x(b, 0)
                if n is not None:
                    q_lo(n, 0)
                    q_lo(n, 1)
                if b is not None:
                    x_lo(b, 0)
                    residual(b, 1)
                if f is not None:
                    finish(f, 1)
                if b is not None:
                    norm_x(b, 1)
                if f is None:
                    split(5)

            for m in (we_h, we_l, m_h, m_l, et_h, et_l, e2_h, e2_l):
                nc.vector.memset(m[64:P, :].bitcast(F32), 0.0)
            nc.vector.memset(arrows[:, NA:NA + TOPK], LARGEST)
            nc.vector.memset(k_stack[QSTACK:P, :, :].bitcast(F32), 1.0).then_inc(const_dve, 1)
            dve.wait_ge(const_dve, 1)

            dve.wait_ge(set_act, 1)
            nc.vector.tensor_tensor(we_l[0:EA, :], w_emb[0:EA, :], we_h[0:EA, :].bitcast(F32),
                                    ALU.subtract).then_inc(set_dve, 1)
            nc.vector.tensor_reduce(out=w_mean[0:EA, 0:1], in_=w_emb[0:EA, :], axis=AX.X, op=ALU.add).then_inc(set_dve, 1)
            dve.wait_ge(set_dve, 2)
            nc.vector.tensor_scalar(w_mean[0:EA, 1:2], w_mean[0:EA, 0:1], 1.0 / D, None, ALU.mult).then_inc(set_dve, 1)
            dve.wait_ge(set_dve, 3)
            nc.vector.tensor_scalar(wc[0:EA, :], w_emb[0:EA, :], w_mean[0:EA, 1:2], None, ALU.subtract).then_inc(set_dve, 1)
            e_lo(0)
            norm_stats(0)
            dve.wait_ge(set_act, 4)
            nc.vector.scalar_tensor_tensor(out=m_l[0:EA, 0:D], in0=ps_vec[0:EA, 1, :], scalar=QSCALE,
                                           in1=m_h[0:EA, 0:D].bitcast(F32), op0=ALU.mult, op1=ALU.subtract).then_inc(set_dve, 1)
            nc.vector.tensor_tensor(m_l[0:EA, D:QKV], ps_vec[0:EA, 2, 0:QKV - D], m_h[0:EA, D:QKV].bitcast(F32),
                                    ALU.subtract).then_inc(set_dve, 1)
            e_scale(0)
            e2_lo(0)
            k_lo(0)
            for i in range(2):
                q_lo(0, i)
            split(0)
            split(1)
            iteration(0, None, 1)
            iteration(1, 0, 2)
            with dve.Fori(2, NB - 1) as b:
                iteration(b, b - 1, b + 1)
            iteration(NB - 1, NB - 2, None)
            iteration(None, NB - 1, None)

        @block.tensor
        def _(pe):
            def passes(dst, chunks):
                n = 3 * len(chunks)
                i = 0
                for l_h, l_l, r_h, r_l in chunks:
                    for lhs, rhs in ((l_h, r_h), (l_h, r_l), (l_l, r_h)):
                        mm = nc.tensor.matmul(dst, lhs, rhs, start=(i == 0), stop=(i == n - 1))
                        i += 1
                return mm

            def e_turn(b):
                after(pe, gathered, b, 16 * TT, 16 * TT)
                after(pe, kl_ready, b - 1, 1, 1)
                for t in range(TT):
                    mm = nc.tensor.transpose(ps_small[0:EA, t * P:(t + 1) * P], e_tok[:, t, :], ident[:, :])
                mm.then_inc(et_done, 1)

            def h0_product(b, t):
                if t == 0:
                    after(pe, etl_ready, b, 1, 1)
                    after(pe, ql_ready, b - 1, 2, 2)
                    after(pe, routed_ready, b - 2, TT, 1)
                else:
                    after(pe, h0_ready, b, TT, 1)
                tok = slice(t * P, (t + 1) * P)
                passes(ps_vec[:, 0, :], [(et_h[:, tok], et_l[:, tok], we_h[:, :], we_l[:, :])]).then_inc(h0_done, 1)

            def e2_turn(b):
                after(pe, e2_ready, b, TT, TT)
                after(pe, utl_ready, b - 2, 2 * TT, 2 * TT)
                for t in range(TT):
                    mm = nc.tensor.transpose(ps_turn[0:EA, t * P:(t + 1) * P], e_scaled[:, t, :], ident[:, :])
                mm.then_inc(e2t_done, 1)

            def k_product(b):
                after(pe, e2l_ready, b, 1, 1)
                after(pe, exp_ready, b - 1, 3 * KV, 3 * KV)
                cols = slice(D, D + KD)
                passes(ps_small[:, 0:S], [(m_h[:, cols], m_l[:, cols], e2_h[:, :], e2_l[:, :])]).then_inc(k_done, 1)

            def q_product(b, i):
                if i == 0:
                    after(pe, h0_ready, b, TT, TT)
                else:
                    after(pe, o_ready, b - 1, KV, KV)
                for c in range(2):
                    cols = slice((2 * i + c) * P, (2 * i + c + 1) * P)
                    mm = passes(ps_vec[:, i, c * S:(c + 1) * S], [(m_h[:, cols], m_l[:, cols], e2_h[:, :], e2_l[:, :])])
                mm.then_inc(q_done, 1)

            def v_product(b):
                for t in range(TT):
                    tok = slice(t * P, (t + 1) * P)
                    mm = passes(ps_vec[:, 2, t * 2 * KD:(t + 1) * 2 * KD],
                                [(e2_h[:, tok], e2_l[:, tok], m_h[:, D:QKV], m_l[:, D:QKV])])
                mm.then_inc(v_done, 1)

            def score(b, n):
                g, c = heads[n]
                if max(g, c) ** 2 == n:
                    after(pe, stacked[max(g, c)], b, n_stack, n_stack)
                if n < 2:
                    after(pe, h1_ready, b - 1, TT, n + 1)
                else:
                    after(pe, max_ready, b, HEADS, n - 1)
                for t in range(TT):
                    mm = nc.tensor.matmul(ps_pair[:, n % 2, t * S:(t + 1) * S],
                                          q_stack[0:QSTACK, t, g, c, :], k_stack[0:QSTACK, c, :],
                                          start=True, stop=True)
                mm.then_inc(s_done, 1)

            def max_turn(b, n):
                after(pe, max_ready, b, HEADS, HEADS)
                if n is not None:
                    after(pe, h0_ready, n, TT, TT)
                nc.tensor.transpose(ps_vec[0:TT * HEADS, 0, 0:P], row_max[:, :, :].rearrange("p t h -> p (t h)"),
                                    ident[:, :]).then_inc(mt_done, 1)

            def scores_t(b, f, n, c):
                if c == 0:
                    after(pe, m_stacked, b, n_mrow, n_mrow)
                for i in range(2):
                    if c > 0:
                        after(pe, exp_ready, b, 3 * KV, 3 * (c - 1) + i + 1)
                    nc.tensor.matmul(ps_pair[:, i, :], k_stack[0:STACK, c, 0:P],
                                     q_stack[0:STACK, :, 2 * i:2 * i + 2, c, :].rearrange("p t g q -> p g t q"),
                                     start=True, stop=True)
                    nc.tensor.matmul(ps_pair[:, i, :].rearrange("p (g q) -> p g q", g=2)[:, :, 0:P], ident_b[:, :],
                                     mask_t[:, :].unsqueeze(1).broadcast_to([P, 2, P]), start=False, stop=True,
                                     skip_group_check=True).then_inc(st_done, 1)
                if c > 0:
                    after(pe, exp_ready, b, 3 * KV, 3 * c)
                elif f is not None:
                    after(pe, utl_ready, f, 2 * TT, 2 * TT)
                elif n is not None:
                    after(pe, etl_ready, n, 1, 1)
                nc.tensor.matmul(ps_small[:, :], k_stack[0:STACK, c, P:S], q_stack[0:STACK, 1, :, c, :],
                                 start=True, stop=False)
                nc.tensor.matmul(ps_small[:, :], ident_b[:, :], mask_t[:, :].unsqueeze(1).broadcast_to([P, GROUP, P]),
                                 start=False, stop=True).then_inc(st_done, 1)

            def values(b, f, c):
                after(pe, exp_ready, b, 3 * KV, 3 * c + 3)
                if c == 0:
                    after(pe, v_ready, b, 1, 1)
                    if f is not None:
                        after(pe, routed_ready, f, TT, TT)
                elif c > 1:
                    after(pe, o_ready, b, KV, c - 1)
                od = ps_vec[:, 2 - c % 2, :]
                for what in range(2):
                    for t in range(TT):
                        for g in range(GROUP):
                            rows = slice(HD * g, HD * (g + 1))
                            lhs = v_tok[:, t, HD * c:HD * (c + 1)] if what == 0 else ones[:, :]
                            rhs = prob0[:, c % 2, g, :] if t == 0 else prob1[:, c % 2, g, :]
                            mm = nc.tensor.matmul(od[rows, what * S + t * P:(what + 1) * S], lhs, rhs,
                                                  start=(t == 0), stop=(t == 1), tile_position=(0, HD * g))
                mm.then_inc(pv_done, 1)

            def out_chunk(b, t, c):
                if t == 0:
                    after(pe, otl_ready, b, KV, c + 1)
                tok = slice(t * P, (t + 1) * P)
                w = slice(c * D, (c + 1) * D)
                for j, (lhs, rhs) in enumerate(((ot_h, wo_h), (ot_h, wo_l), (ot_l, wo_h))):
                    mm = nc.tensor.matmul(ps_pair[:, t, :], lhs[:, c, tok], rhs[:, w], start=(c == 0 and j == 0),
                                          stop=(c == DC - 1 and j == 2))
                if c == DC - 1:
                    mm.then_inc(wo_done, 1)

            def x_turn(f, t):
                after(pe, x_ready, f, TT, t + 1)
                if t == 0:
                    after(pe, utl_ready, f - 1, 2 * TT, 2 * TT)
                else:
                    after(pe, xl_ready, f, TT, 1)
                for c in range(DC):
                    mm = nc.tensor.transpose(ps_turn[:, c * P:(c + 1) * P], x[:, t, c * P:(c + 1) * P], ident[:, :])
                mm.then_inc(xt_done, 1)

            def vec_chunk(f, b, t, i):
                half, c = divmod(i, DC)
                n = half if t == 0 else 1 - half
                if i == 0:
                    after(pe, xl_ready, f, TT, t + 1)
                if c == 0:
                    if (t, half) == (1, 1):
                        after(pe, routed_ready, f, TT, 1)
                    elif b is None:
                        after(pe, o_ready, f, KV, KV)
                    elif t == 0:
                        after(pe, ql_ready, b, 2, half + 1)
                    else:
                        after(pe, v_ready, b, 1, 1)
                w = slice(c * AR + n * 512, c * AR + (n + 1) * 512)
                for j, (lhs, rhs) in enumerate(((xt_h, at_h), (xt_h, at_l), (xt_l, at_h))):
                    mm = nc.tensor.matmul(ps_vec[:, t + n, :], lhs[:, t, c, :], rhs[:, w], start=(c == 0 and j == 0),
                                          stop=(c == DC - 1 and j == 2))
                if c == DC - 1:
                    mm.then_inc(vec_done, 1)

            def base_part(f, t, parts):
                for i in parts:
                    c, j = divmod(i, 3)
                    if i == 0:
                        after(pe, result_ready, f, TT, t)
                    lhs, rhs = ((xt_h, wt_h), (xt_h, wt_l), (xt_l, wt_h))[j]
                    nc.tensor.matmul(ps_acc[:, :], lhs[:, t, c, :], rhs[:, c * D:(c + 1) * D], start=(i == 0), stop=False)

            def u_turn(f, b, n, t, h):
                if h == 0:
                    after(pe, u_ready, f, TT, t + 1)
                if t == 1:
                    after(pe, utl_ready, f, 2 * TT, 2 * t + h - 1)
                elif h == 0:
                    after(pe, xl_ready, f, TT, TT)
                elif n is not None:
                    after(pe, etl_ready, n, 1, 1)
                elif b is not None:
                    after(pe, kl_ready, b, 1, 1)
                for i in range(4):
                    k = 4 * h + i
                    mm = nc.tensor.transpose((ps_turn, ps_small)[h][:, i * P:(i + 1) * P], u[:, k * P:(k + 1) * P],
                                             ident[:, :])
                mm.then_inc(ut_done, 1)

            def delta_chunk(f, t, k):
                if k % 4 == 0:
                    after(pe, utl_ready, f, 2 * TT, 2 * t + k // 4 + 1)
                if isinstance(f, int) and (f, t, k) == (0, 0, 0):
                    pe.wait_ge(part_lo, len(pieces))
                w = slice(k * D, (k + 1) * D)
                for j, (lhs, rhs) in enumerate(((ut_h, bt_h), (ut_h, bt_l), (ut_l, bt_h))):
                    mm = nc.tensor.matmul(ps_acc[:, :], lhs[:, k, :], rhs[:, w], start=False,
                                          stop=(k == RC - 1 and j == 2))
                if k == RC - 1:
                    mm.then_inc(acc_done, 1)

            def iteration(b, f, n):
                if n is not None:
                    e_turn(n)
                if f is not None:
                    for i in range(2 * DC):
                        vec_chunk(f, b, 0, i)
                        if i == 4:
                            x_turn(f, 1)
                    base_part(f, 0, range(3 * DC if b is not None else DC))
                    for i in range(DC):
                        vec_chunk(f, b, 1, i)
                if b is not None:
                    score(b, 0)
                    score(b, 1)
                for i in range(DC):
                    if f is not None:
                        vec_chunk(f, b, 1, DC + i)
                    if b is not None:
                        score(b, 2 + i)
                for h in range(2):
                    if f is not None:
                        u_turn(f, b, n, 0, h)
                    if b is not None:
                        score(b, 6 + h)
                if b is None:
                    base_part(f, 0, range(DC, 3 * DC))
                if n is not None:
                    h0_product(n, 0)
                if b is not None:
                    score(b, 8)
                for i in range(3):
                    if f is not None:
                        delta_chunk(f, 0, 2 * i)
                        delta_chunk(f, 0, 2 * i + 1)
                    if b is not None:
                        score(b, 9 + i)
                if f is not None:
                    delta_chunk(f, 0, 6)
                    delta_chunk(f, 0, 7)
                if n is not None:
                    h0_product(n, 1)
                if f is not None:
                    base_part(f, 1, range(0, 3))
                for i in range(12, HEADS):
                    if b is not None:
                        score(b, i)
                    if f is not None:
                        base_part(f, 1, range(i - 8, i - 7) if i > 12 else range(3, 5))
                if f is not None:
                    u_turn(f, b, n, 1, 0)
                if b is not None:
                    max_turn(b, n)
                if f is not None:
                    u_turn(f, b, n, 1, 1)
                    base_part(f, 1, range(8, 3 * DC))
                    for k in range(0, 4):
                        delta_chunk(f, 1, k)
                if b is not None:
                    scores_t(b, f, n, 0)
                if f is not None:
                    delta_chunk(f, 1, 4)
                if b is not None:
                    scores_t(b, f, n, 1)
                    values(b, f, 0)
                if n is not None:
                    e2_turn(n)
                if b is not None:
                    scores_t(b, f, n, 2)
                    values(b, f, 1)
                    scores_t(b, f, n, 3)
                    values(b, f, 2)
                    values(b, f, 3)
                    for c in range(2):
                        for t in range(TT):
                            out_chunk(b, t, c)
                if n is not None:
                    k_product(n)
                    q_product(n, 0)
                if b is not None:
                    for t in range(TT):
                        for c in range(2, DC):
                            out_chunk(b, t, c)
                if n is not None:
                    q_product(n, 1)
                    v_product(n)
                if f is not None:
                    delta_chunk(f, 1, 5)
                if b is not None:
                    x_turn(b, 0)
                if f is not None:
                    for k in range(6, RC):
                        delta_chunk(f, 1, k)

            pe.wait_ge(const_pool, 11)
            pe.wait_ge(const_dve, 1)
            pe.wait_ge(set_dve, 4)
            for c in range(DC):
                mm = nc.tensor.transpose(ps_turn[:, c * P:c * P + EA], wc[0:EA, c * P:(c + 1) * P], ident[0:EA, 0:EA])
            mm.then_inc(set_pe, 1)
            pe.wait_ge(set_act, 2)
            pe.wait_ge(qkv_in, 48)
            for n, w in enumerate((w_query, w_kv)):
                if n == 1:
                    e_turn(0)
                    h0_product(0, 0)
                    h0_product(0, 1)
                for c in range(DC):
                    mm = nc.tensor.matmul(ps_vec[0:EA, 1 + n, 0:w.shape[2]], wc_t[:, c, 0:EA], w[:, c, :],
                                          start=(c == 0), stop=(c == DC - 1))
            mm.then_inc(set_pe, 1)
            e2_turn(0)
            pe.wait_ge(set_dve, 6)
            k_product(0)
            for i in range(2):
                q_product(0, i)
            v_product(0)
            pe.wait_ge(part_lo, 1)
            iteration(0, None, 1)
            pe.wait_ge(part_lo, 4)
            iteration(1, 0, 2)
            with pe.Fori(2, NB - 1) as b:
                iteration(b, b - 1, b + 1)
            iteration(NB - 1, NB - 2, None)
            iteration(None, NB - 1, None)


def kernel(x, L0_tok_emb, L0_tok_W, L0_tok_b, L0_attn_Wq, L0_attn_Wk, L0_attn_Wv, L0_attn_Wo,
           L0_ffn_A, L0_ffn_B, L0_ffn_W, L0_ffn_bias):
    import numpy as np
    import concourse.bacc as bacc
    from concourse.bass_utils import run_bass_kernel_spmd

    x = np.asarray(x)
    A = np.asarray(L0_ffn_A)
    B = np.asarray(L0_ffn_B)
    arrays = {
        "ids": np.ascontiguousarray(x.reshape(-1, 128).T),
        "emb": np.ascontiguousarray(L0_tok_emb),
        "w_tok": np.ascontiguousarray(L0_tok_W),
        "b_tok": np.ascontiguousarray(L0_tok_b),
        "w_q": np.ascontiguousarray(L0_attn_Wq),
        "w_k": np.ascontiguousarray(L0_attn_Wk),
        "w_v": np.ascontiguousarray(L0_attn_Wv),
        "w_o": np.ascontiguousarray(L0_attn_Wo),
        "a_t": np.ascontiguousarray(A.reshape(-1, A.shape[2]).T),
        "b_t": np.ascontiguousarray(B.transpose(0, 2, 1).reshape(-1, B.shape[1])),
        "w_t": np.ascontiguousarray(np.asarray(L0_ffn_W).T),
        "bias": np.ascontiguousarray(L0_ffn_bias),
    }
    nc = bacc.Bacc("TRN2", target_bir_lowering=False, num_devices=1)
    args = [nc.dram_tensor(n, a.shape, mybir.dt.from_np(a.dtype), kind="ExternalInput").ap() for n, a in arrays.items()]
    out = nc.dram_tensor("out", (x.size, L0_tok_W.shape[1]), F32, kind="ExternalOutput").ap()
    tower_kernel(nc, *args, out)
    r = run_bass_kernel_spmd(nc, [arrays], core_ids=[0])
    return r.results[0]["out"].reshape(*x.shape, -1)
```
